# Optimizing a Trainium2 kernel written in Bass

```python
import numpy as np
import jax
import jax.numpy as jnp

def _softmax(x, axis=-1):
    return jax.nn.softmax(x, axis=axis)

def _gelu(x):
    return jax.nn.gelu(x, approximate=True)

def _silu(x):
    return jax.nn.silu(x)

def _sigmoid(x):
    return jax.nn.sigmoid(x)

def _layernorm(x, axis=-1, eps=1e-05):
    m = jnp.mean(x, axis=axis, keepdims=True)
    v = jnp.var(x, axis=axis, keepdims=True)
    return (x - m) / jnp.sqrt(v + eps)

def _scatter_add(tgt, idx, src, axis=0):
    return tgt.at[idx].add(src)

def _segment_sum(src, seg, n):
    return jax.ops.segment_sum(src, seg, n)
kernel_name = 'mk_adj_resnorm_d1_adj_r2_b0c785'

def setup_inputs(seed: int=0):
    np.random.seed(seed)
    _w = jnp.asarray

    def _rec_inputs():
        import jax
        import jax.numpy as jnp
        _gk = jax.random.key(seed)
        x = -0.0005207 + 1.001 * jax.random.normal(jax.random.fold_in(_gk, 1), (4096, 128), jnp.float32)
        _a = jax.random.bernoulli(jax.random.fold_in(_gk, 2), 0.00390625, (4096, 4096))
        _a = jnp.logical_or(_a, jnp.swapaxes(_a, -1, -2))
        _a = jnp.logical_or(_a, jnp.eye(4096, dtype=bool))
        adj = _a.astype(jnp.int32)
        return (x, adj)
    x, adj = _rec_inputs()

    def _L0_gnn_setup():
        import jax, jax.numpy as jnp
        import numpy as np
        N = 4096
        IN_CH = 128
        HID = 128
        NEG_INF = -1000000000.0
        key = jax.random.key(seed)
        ks = jax.random.split(key, 7)
        inlayer = jax.random.normal(ks[0], (N, IN_CH), dtype=jnp.float32)
        adj_mat = jax.random.randint(ks[1], (N, N), 0, 2, dtype=jnp.int32)
        s0 = (6.0 / (IN_CH + HID)) ** 0.5
        s1 = (6.0 / (HID + 1)) ** 0.5
        W = jax.random.uniform(ks[2], (HID, IN_CH), jnp.float32, -s0, s0)
        w1 = jax.random.uniform(ks[3], (1, HID), jnp.float32, -s1, s1)
        b1 = jax.random.uniform(ks[4], (1,), jnp.float32, -s1, s1)
        w2 = jax.random.uniform(ks[5], (1, HID), jnp.float32, -s1, s1)
        b2 = jax.random.uniform(ks[6], (1,), jnp.float32, -s1, s1)
        return {'inlayer': inlayer, 'adj_mat': adj_mat, 'W': W, 'w1': w1, 'b1': b1, 'w2': w2, 'b2': b2}
    _L0_gnn_all = _L0_gnn_setup()
    _L0_gnn_in = {k: v for k, v in _L0_gnn_all.items() if k in ('W', 'w1', 'b1', 'w2', 'b2')}
    del _L0_gnn_all
    return {'x': x, 'adj': adj, 'L0_gnn_W': _L0_gnn_in['W'], 'L0_gnn_w1': _L0_gnn_in['w1'], 'L0_gnn_b1': _L0_gnn_in['b1'], 'L0_gnn_w2': _L0_gnn_in['w2'], 'L0_gnn_b2': _L0_gnn_in['b2']}

def reference(x, adj, L0_gnn_W, L0_gnn_w1, L0_gnn_b1, L0_gnn_w2, L0_gnn_b2):
    import jax
    import jax.numpy as jnp

    def _L0_gnn_ref(inlayer, adj_mat, W, w1, b1, w2, b2):
        import jax, jax.numpy as jnp
        import numpy as np
        N = 4096
        IN_CH = 128
        HID = 128
        NEG_INF = -1000000000.0
        in_fts = W @ inlayer.T
        f1 = (w1 @ in_fts).T + b1
        f2 = (w2 @ in_fts).T + b2
        logits = f1 + f2.T
        bias_mat = jnp.where(adj_mat > 0, 0.0, NEG_INF).astype(logits.dtype)
        coefs = jax.nn.softmax(jax.nn.leaky_relu(logits) + bias_mat, axis=-1)
        vals = coefs @ inlayer
        return vals
    x = _layernorm(x + _L0_gnn_ref(x, adj, L0_gnn_W, L0_gnn_w1, L0_gnn_b1, L0_gnn_w2, L0_gnn_b2), axis=-1)
    return x

_drawn_inputs = setup_inputs


def setup_inputs(seed=0):
    import zlib

    import numpy as np

    out = dict(_drawn_inputs(seed))
    spreads = {}
    factors = {}
    for name, (base, spread) in spreads.items():
        noise = np.random.default_rng([zlib.crc32(name.encode()), seed]).standard_normal(out[name].shape)
        drawn = base * np.exp(spread * noise) if base else spread * noise
        out[name] = jnp.asarray(drawn.astype(out[name].dtype))
    for name, factor in factors.items():
        out[name] = (out[name] * factor).astype(out[name].dtype)
    return out
```

```python
from contextlib import ExitStack

import concourse.bass as bass
from concourse import mybir

ALU = mybir.AluOpType
ACT = mybir.ActivationFunctionType
F32 = mybir.dt.float32
F16 = mybir.dt.float16
FP8 = mybir.dt.float8e5
I32 = mybir.dt.int32
U32 = mybir.dt.uint32
U8 = mybir.dt.uint8
I8 = mybir.dt.int8
AX_X = mybir.AxisListType.X

P = 128
SQ = 32
NEG_SLOPE = 0.01
NEG_INF = 1.0e9
EPS = 1.0e-5
SCALE = 1024.0
PAT_MIN = 2.0 ** -14

F2_SPAN = 17.0
F_ABS = 31.0
X_MAX = 30.0
X_MIN = 2.0 ** -6


def gat_kernel(nc, x, adj, W, w1, b1, w2, b2, out):
    N, D = x.shape
    NT = N // P
    QT = 4
    NQ = NT // QT
    A = P // SQ
    JA = N // A
    KB = 4
    NB = JA // (SQ * KB)
    NK = NB * KB
    G = P // SQ
    DV = D + 1
    XG = 4
    NXG = NT // XG
    BCH = 4
    CN = NK // BCH
    PW = 2 * P
    QW = QT * P

    adj_v = adj.rearrange("(t g s) (a c) -> t a s g c", g=G, s=SQ, a=A)
    x_rows = x.rearrange("(t p) d -> p t d", p=P)
    x_cols = x.rearrange("(a b r k) d -> a r b (k d)", a=A, b=NB, r=SQ)
    out_q = out.rearrange("(q c p) d -> q p c d", c=QT, p=P)
    adj_t = adj.rearrange("(t p) j -> t p j", p=P)
    out_t = out.rearrange("(t p) d -> t p d", p=P)

    with ExitStack() as ctx:
        def sb(name, shape, dt):
            return ctx.enter_context(nc.sbuf_tensor(name, shape, dt))

        def sem(name):
            return ctx.enter_context(nc.semaphore(name))

        xn = sb("xn", [P, NT, D], F32)
        f1b = sb("f1b", [P, N], F32)
        f12 = sb("f12", [P, NT, 2], F32)
        f2l = sb("f2l", [P, NK], F32)
        nf2l = sb("nf2l", [P, NK], F32)
        wsb = sb("wsb", [P, D], F32)
        w12 = sb("w12", [P, 2], F32)
        b12 = sb("b12", [P, 2], F32)
        wbc = sb("wbc", [P, 2, P], F32)
        vsb = sb("vsb", [P, 2 * P + 2], F32)
        ident = sb("ident", [P, P], F32)
        ones = sb("ones", [P, P], F32)
        stat = sb("stat", [P, 4], F32)
        stmax = sb("stmax", [4, 1], F32)
        stdiag = sb("stdiag", [4, 4], F32)
        gst = sb("gst", [P, 4], F32)
        rng = sb("rng", [P, 4], F32)
        flag = sb("flag", [P, 1], I32)
        nF2 = sb("nF2", [P, 1], F32)

        nat = sb("nat", [P, 2, G * JA], I32)
        masks = sb("masks", [P, 2, 2, NK * PW], U8)
        mnt = sb("mnt", [P, 2, NK * PW], U8)
        sgn = sb("sgn", [P, 2, NK * QW], I8)
        bt = sb("bt", [P, 2, NK * 2 * DV], F16)
        post = sb("post", [P, 2, 2, QT, 2 * DV], F32)

        xl = masks[:, 1].rearrange("p s n -> p (s n)").bitcast(F32)
        xT = mnt[:, :, :].rearrange("p s n -> p (s n)").bitcast(F32)
        xTp = sgn[:, 0].bitcast(F32)
        ybuf = sgn[:, 1, 0:2 * CN * DV * 4].bitcast(F32).rearrange("p (s n d) -> p s n d", s=2, d=DV)
        mn_w = mnt[:, 0].bitcast(U32)
        mt_w = mnt[:, 1].bitcast(U32).rearrange("p (b i) -> p b i", b=NB)
        sgn_w = [sgn[:, s].bitcast(U32).rearrange("p (b i) -> p b i", b=NB) for s in range(2)]
        sgn_b = [sgn[:, s].rearrange("p (b i k) -> p b i k", b=NB, k=KB) for s in range(2)]
        mask_w = [[masks[:, s, m].bitcast(U32).rearrange("p (b i) -> p b i", b=NB) for m in range(2)]
                  for s in range(2)]
        mask_f = [[masks[:, s, m].bitcast(FP8).rearrange("p (b i k) -> p b k i", b=NB, k=KB)
                   for m in range(2)] for s in range(2)]
        btv = [bt[:, m].rearrange("p (n d) -> p n d", n=NK) for m in range(2)]

        be = sb("be", [P, NK], F32)
        de = sb("de", [P, NK], F32)
        p2 = sb("p2", [P, NK], F32)
        rp = sb("rp", [P, NK], F32)
        cs = sb("cs", [P, 2, NK], F32)
        pat = sb("pat", [P, NK], FP8)
        gsum = sb("gsum", [P, NT], F32)
        mrow = sb("mrow", [P, NT], F32)
        ea = sb("ea", [P, 2, NT], F32)
        ac = sb("ac", [P, 2, NT], F32)
        xsum = sb("xsum", [P, DV], F32)
        ntot = sb("ntot", [P, QT, DV], F32)
        iso = sb("iso", [P, QT], F32)
        den = sb("den", [P, QT], F32)
        rec = sb("rec", [P, QT], F32)
        isox = sb("isox", [P, QT, DV], F32)
        ybt = sb("ybt", [P, 2, QT, D], F32)
        bns = sb("bns", [P, 2, QT, 6], F32)
        mv = sb("mv", [P, 2, QT, 2], F32)
        vpe = sb("vpe", [P, QT], F32)
        mhalf = sb("mhalf", [P, QT], F32)
        rstd = sb("rstd", [P, 2, QT], F32)

        gnmax = sb("gnmax", [P, 1], F32)
        gden = sb("gden", [P, 1], F32)

        ps = ctx.enter_context(nc.psum_tensor("ps", [P, 8, 512], F32))

        weights_in = sem("weights_in")
        xn_in = [sem(f"xn_in{i}") for i in range(4)]
        xl_in = sem("xl_in")
        ident_zero = sem("ident_zero")
        consts_ready = sem("consts_ready")
        wbc_ready = sem("wbc_ready")
        v_made = sem("v_made")
        vsb_ready = sem("vsb_ready")
        x_turned = sem("x_turned")
        xT_ready = sem("xT_ready")
        xTp_ready = sem("xTp_ready")
        f1_made = sem("f1_made")
        f1b_ready = sem("f1b_ready")
        f_made = sem("f_made")
        f12_ready = sem("f12_ready")
        nf2l_ready = sem("nf2l_ready")
        stat_ready = sem("stat_ready")
        stat_turned = sem("stat_turned")
        stmax_ready = sem("stmax_ready")
        diag_ready = sem("diag_ready")
        gst_made = sem("gst_made")
        gst_ready = sem("gst_ready")
        rng_step = sem("rng_step")
        nat_in = [sem(f"nat_in{i}") for i in range(2)]
        exp_ready = sem("exp_ready")
        tab_step = sem("tab_step")
        rows_ready = sem("rows_ready")
        ea_ready = sem("ea_ready")
        y_ready = sem("y_ready")
        hi_ready = sem("hi_ready")
        table_ready = sem("table_ready")
        xsum_made = sem("xsum_made")
        xsum_ready = sem("xsum_ready")
        sign_ready = sem("sign_ready")
        cast_done = sem("cast_done")
        turn_done = sem("turn_done")
        plus_ready = sem("plus_ready")
        minus_ready = sem("minus_ready")
        sums_made = sem("sums_made")
        sums_out = sem("sums_out")
        sums_added = sem("sums_added")
        pool_step = sem("pool_step")
        rec_step = sem("rec_step")
        y_done = sem("y_done")
        bn_step = sem("bn_step")
        mv_ready = sem("mv_ready")
        rstd_ready = sem("rstd_ready")
        out_ready = sem("out_ready")
        out_stored = [sem(f"out_stored{i}") for i in range(2)]
        g_adj_in = sem("g_adj_in")
        g_f2_made = sem("g_f2_made")
        g_f2_ready = sem("g_f2_ready")
        g_step = sem("g_step")
        g_max_ready = sem("g_max_ready")
        g_exp_ready = sem("g_exp_ready")
        g_turned = sem("g_turned")
        g_pt_ready = sem("g_pt_ready")
        g_sum_made = sem("g_sum_made")
        g_out_ready = sem("g_out_ready")
        g_rstd = sem("g_rstd")
        g_stored = sem("g_stored")
        flag_ready = sem("flag_ready")

        steps_begun = {e.engine: sem(f"steps_begun_{n}") for n, e in
                       (("pe", nc.tensor), ("dve", nc.vector), ("pool", nc.gpsimd))}

        block = ctx.enter_context(nc.Block())

        def fast(eng):
            eng.wait_ge(flag_ready, 1)
            return eng.value_load(flag[0:1, 0:1], min_val=0, max_val=1)

        def apart(eng):
            eng.sem_inc(steps_begun[eng.engine], 1)

        def quads(eng, body):
            body(0, 0)
            body(1, 1)
            with eng.Fori(1, NQ // 2) as turn:
                body(2 * turn, 0)
                body(2 * turn + 1, 1)

        @block.sync
        def _(sp):
            sp.dma_start(wsb[:, :], W).then_inc(weights_in, 16)
            sp.dma_start(w12[:, 0:1], w1.rearrange("o h -> h o")).then_inc(weights_in, 16)
            sp.dma_start(w12[:, 1:2], w2.rearrange("o h -> h o")).then_inc(weights_in, 16)
            sp.dma_start(b12[:, 0:1], b1.partition_broadcast(P)).then_inc(weights_in, 16)
            sp.dma_start(b12[:, 1:2], b2.partition_broadcast(P)).then_inc(weights_in, 16)
            for i in range(4):
                part = slice(i * NT // 4, (i + 1) * NT // 4)
                sp.dma_start(xn[:, part, :], x_rows[:, part, :]).then_inc(xn_in[i], 16)
            for a in range(A):
                sp.dma_start(xl[a * SQ:(a + 1) * SQ, :].rearrange("r (b n) -> r b n", b=NB),
                             x_cols[a]).then_inc(xl_in, 16)

            def load_adj(t, slot):
                for a in range(A):
                    dst = nat[a * SQ:(a + 1) * SQ, slot, :].rearrange("s (g c) -> s g c", g=G)
                    sp.dma_start(dst, adj_v[t, a]).then_inc(nat_in[slot], 16)

            load_adj(0, 0)
            load_adj(1, 1)
            go = fast(sp)
            with sp.If(go):
                def load_quad(q, c0):
                    for c in range(c0, QT):
                        sp.wait_ge(cast_done, QT * q + c - 1)
                        load_adj(QT * q + c, c % 2)

                def store(q, s):
                    sp.wait_ge(out_ready, q + 1)
                    sp.dma_start(out_q[q], ybt[:, s]).then_inc(out_stored[s], 16)

                load_quad(0, 2)
                load_quad(1, 0)
                load_quad(2, 0)
                load_quad(3, 0)
                store(0, 0)
                with sp.Fori(2, NQ // 2) as turn:
                    load_quad(2 * turn, 0)
                    store(2 * turn - 3, 1)
                    load_quad(2 * turn + 1, 0)
                    store(2 * turn - 2, 0)
                for q in (NQ - 3, NQ - 2, NQ - 1):
                    store(q, q % 2)
                for s in range(2):
                    sp.wait_ge(out_stored[s], 16 * NQ // 2)
            with sp.Else():
                def load_rows(t):
                    sp.dma_start(nat[:, 0, :], adj_t[t]).then_inc(g_adj_in, 16)

                def store_rows(t):
                    sp.wait_ge(g_out_ready, t + 1)
                    sp.dma_start(out_t[t], ybt[:, 1, 0, :]).then_inc(g_stored, 16)

                sp.wait_ge(nat_in[0], 16 * A)
                sp.wait_ge(nat_in[1], 16 * A)
                load_rows(0)
                with sp.Fori(1, NT) as t:
                    sp.wait_ge(g_max_ready, t)
                    load_rows(t)
                    store_rows(t - 1)
                store_rows(NT - 1)
                sp.wait_ge(g_stored, 16 * NT)
            sp.nop()

        @block.gpsimd
        def _(pool):
            pool.memset(ident[:, :], 0.0).then_inc(ident_zero, 1)
            pool.memset(ones[:, :], 1.0)
            pool.memset(mhalf[:, :], -0.5)
            pool.memset(xsum[:, D:DV], float(N))
            pool.wait_ge(ident_zero, 1)
            pool.affine_select(out=ident[:, :], in_=ident[:, :], compare_op=ALU.not_equal, fill=1.0,
                               base=0, pattern=[[-1, P]], channel_multiplier=1).then_inc(consts_ready, 1)
            go = fast(pool)
            with pool.If(go):
                for m in range(2):
                    for h in range(BCH):
                        i = m * BCH + h
                        part = slice(h * CN, (h + 1) * CN)
                        pool.wait_ge(hi_ready, i + 1)
                        pool.tensor_tensor(btv[m][:, part, DV:2 * DV], ybuf[:, i % 2], btv[m][:, part, 0:DV],
                                           ALU.subtract).then_inc(table_ready, 1)

                def quad(q, s):
                    pool.wait_ge(sums_out, QT * (q + 1))
                    pool.tensor_tensor(post[:, s, 0], post[:, s, 0], post[:, s, 1],
                                       ALU.add).then_inc(pool_step, 1)
                    pool.wait_ge(pool_step, 5 * q + 1)
                    pool.tensor_tensor(ntot[:, :, :], post[:, s, 0, :, 0:DV], post[:, s, 0, :, DV:2 * DV],
                                       ALU.add).then_inc(sums_added, 1)
                    pool.wait_ge(rec_step, 3 * q + 3)
                    pool.wait_ge(xsum_ready, 1)
                    pool.tensor_tensor(isox[:, :, :], xsum[:, None, :].to_broadcast([P, QT, DV]),
                                       iso[:, :, None].to_broadcast([P, QT, DV]),
                                       ALU.mult).then_inc(pool_step, 1)
                    pool.wait_ge(pool_step, 5 * q + 2)
                    pool.tensor_tensor(ntot[:, :, :], ntot[:, :, :], isox[:, :, :], ALU.add).then_inc(pool_step, 1)
                    pool.wait_ge(pool_step, 5 * q + 3)
                    if not isinstance(q, int):
                        pool.wait_ge(out_stored[s], 8 * (q - s))
                    pool.tensor_tensor(ybt[:, s], ntot[:, :, 0:D],
                                       rec[:, :, None].to_broadcast([P, QT, D]),
                                       ALU.mult).then_inc(pool_step, 1)
                    pool.wait_ge(pool_step, 5 * q + 4)
                    pool.tensor_tensor(ybt[:, s], ybt[:, s], xn[:, bass.ds(QT * q, QT), :],
                                       ALU.add).then_inc(y_done, 1)
                    pool.wait_ge(mv_ready, q + 1)
                    apart(pool)
                    pool.tensor_scalar(vpe[:, :], mv[:, s, :, 1], EPS, None, ALU.add).then_inc(pool_step, 1)
                    pool.wait_ge(pool_step, 5 * q + 5)
                    pool.tensor_tensor(rstd[:, s], vpe[:, :], mhalf[:, :], ALU.pow).then_inc(rstd_ready, 1)

                quads(pool, quad)
            with pool.Else():
                with pool.Fori(0, NT) as t:
                    pool.wait_ge(mv_ready, t + 1)
                    apart(pool)
                    pool.tensor_scalar(vpe[:, 0:1], mv[:, 0, 0, 1:2], EPS, None, ALU.add).then_inc(pool_step, 1)
                    pool.wait_ge(pool_step, t + 1)
                    pool.tensor_tensor(rstd[:, 0, 0:1], vpe[:, 0:1], mhalf[:, 0:1], ALU.pow).then_inc(g_rstd, 1)
            pool.nop()

        @block.scalar
        def _(act):
            act.wait_ge(weights_in, 80)
            xTp_v = xTp.rearrange("c (b k a r) -> c a b r k", b=NB, k=KB, a=A)
            bg = NB * A // NXG
            for g in range(NXG):
                act.wait_ge(xT_ready, g + 1)
                act.activation(xTp_v[:, g * bg // NB, g * bg % NB:g * bg % NB + bg],
                               xT[:, g * 512:(g + 1) * 512].rearrange("c (b r k) -> c b r k", b=bg, r=SQ),
                               ACT.Copy).then_inc(xTp_ready, 1)
                act.wait_ge(f1_made, g + 1)
                act.activation(f1b[:, g * 512:(g + 1) * 512], ps[:, 2 + g % 2, :], ACT.Identity,
                               bias=b12[:, 0:1]).then_inc(f1b_ready, 1)
            go = fast(act)
            with act.If(go):
                act.activation(be[:, :], f2l[:, :], ACT.Exp, bias=nF2[:, 0:1]).then_inc(exp_ready, 1)
                act.activation(de[:, :], f2l[:, :], ACT.Exp, scale=NEG_SLOPE).then_inc(exp_ready, 1)
                act.wait_ge(ea_ready, 1)
                act.activation(ac[:, :, :], ea[:, :, :], ACT.Exp).then_inc(rows_ready, 1)
                act.wait_ge(rows_ready, 1)

                def signs(q, s, b0, b1):
                    for b in range(b0, b1):
                        for k in range(KB):
                            n = b * KB + k
                            ins = act.activation(sgn_b[s][:, b, :, k], f1b[:, bass.ds(q * QW, QW)], ACT.Sign,
                                                 bias=nf2l[:, n:n + 1], scale=-1.0)
                        ins.then_inc(sign_ready, 1)

                for i in range(2 * BCH):
                    part = slice((i % BCH) * CN, (i % BCH + 1) * CN)
                    act.wait_ge(y_ready, i + 1)
                    act.activation(btv[i // BCH][:, part, 0:DV], ybuf[:, i % 2], ACT.Copy).then_inc(hi_ready, 1)
                    signs(0, 0, i, i + 1)
                act.wait_ge(xsum_made, 1)
                act.activation(xsum[:, 0:D], ps[:, 7, 0:D], ACT.Copy).then_inc(xsum_ready, 1)

                def evacuate(q, s, c):
                    act.wait_ge(sums_made, QT * q + c + 1)
                    if c == 0 and not (isinstance(q, int) and q < 2):
                        act.wait_ge(sums_added, q - 1)
                    for m in range(2):
                        ins = act.activation(post[:, s, m, c, :], ps[:, 2 * (c % 2) + m, 0:2 * DV], ACT.Copy,
                                             scale=ac[:, m, bass.ds(QT * q + c, 1)])
                    ins.then_inc(sums_out, 1)

                def quad(q, s, more=True):
                    for c, (b0, b1) in enumerate(((0, 3), (3, 6), (6, 8), (8, 8))):
                        if more and b1 > b0:
                            if c == 0:
                                if isinstance(q, int) and q == 0:
                                    act.wait_ge(table_ready, 2 * BCH)
                                else:
                                    act.wait_ge(minus_ready, 2 * q)
                            signs(q + 1, 1 - s, b0, b1)
                        evacuate(q, s, c)

                quad(0, 0)
                quad(1, 1)
                with act.Fori(1, NQ // 2 - 1) as turn:
                    quad(2 * turn, 0)
                    quad(2 * turn + 1, 1)
                quad(NQ - 2, 0)
                quad(NQ - 1, 1, more=False)

            with act.Else():
                P_nat = sgn[:, 0].bitcast(F32)
                with act.Fori(0, NT) as t:
                    act.wait_ge(g_max_ready, t + 1)
                    act.activation(P_nat, P_nat, ACT.Exp, bias=gnmax[:, 0:1],
                                   accum_out=gden[:, 0:1]).then_inc(g_exp_ready, 1)
            act.nop()

        @block.vector
        def _(dve):
            dve.wait_ge(weights_in, 80)
            dve.wait_ge(consts_ready, 1)
            for m in range(2):
                dve.tensor_scalar(wbc[:, m, :], ones[:, :], w12[:, m:m + 1], None, ALU.mult).then_inc(wbc_ready, 1)
            dve.wait_ge(v_made, 1)
            dve.tensor_copy(vsb[:, :], ps[:, 4, 0:2 * P + 2]).then_inc(vsb_ready, 1)
            for g in range(NXG):
                dve.wait_ge(x_turned, g + 1)
                dve.tensor_copy(xT[:, g * 512:(g + 1) * 512], ps[:, g % 2, :]).then_inc(xT_ready, 1)
            dve.tensor_reduce(stat[:, 3:4], xn[:, :, :].rearrange("p t d -> p (t d)"), AX_X, ALU.max,
                              apply_absolute_value=True)
            dve.wait_ge(f_made, 1)
            dve.tensor_tensor(f12[:, :, :], ps[:, 5, 0:2 * NT].rearrange("p (t m) -> p t m", m=2),
                              b12[:, None, :].to_broadcast([P, NT, 2]), ALU.add).then_inc(f12_ready, 1)
            dve.tensor_scalar(f2l[:, :], ps[:, 6, 0:NK], b12[:, 1:2], None, ALU.add).then_inc(f12_ready, 1)
            dve.wait_ge(f12_ready, 2)
            dve.tensor_scalar(nf2l[:, :], f2l[:, :], -1.0, None, ALU.mult).then_inc(nf2l_ready, 1)
            dve.tensor_reduce(stat[:, 0:1], f12[:, :, 1], AX_X, ALU.max)
            dve.tensor_reduce(stat[:, 1:2], f12[:, :, 1], AX_X, ALU.min, negate=True)
            dve.tensor_reduce(stat[:, 2:3], f12[:, :, 0], AX_X, ALU.max,
                              apply_absolute_value=True).then_inc(stat_ready, 1)
            dve.wait_ge(stat_turned, 1)
            dve.tensor_reduce(stmax[:, :], ps[0:4, 7, 0:P], AX_X, ALU.max).then_inc(stmax_ready, 1)
            dve.wait_ge(stmax_ready, 1)
            dve.tensor_scalar(stdiag[:, :], ident[0:4, 0:4], stmax[:, 0:1], None, ALU.mult).then_inc(diag_ready, 1)
            dve.wait_ge(gst_made, 1)
            dve.tensor_copy(gst[:, :], ps[:, 7, 256:260]).then_inc(gst_ready, 1)
            dve.wait_ge(gst_ready, 1)
            dve.tensor_scalar(nF2[:, :], gst[:, 0:1], -1.0, None, ALU.mult)
            dve.tensor_tensor(rng[:, 0:1], gst[:, 0:1], gst[:, 1:2], ALU.add).then_inc(rng_step, 1)
            dve.scalar_tensor_tensor(out=rng[:, 1:2], in0=gst[:, 0:1], scalar=gst[:, 1:2], in1=gst[:, 2:3],
                                     op0=ALU.max, op1=ALU.add).then_inc(rng_step, 1)
            dve.wait_ge(rng_step, 2)
            dve.tensor_scalar(rng[:, 2:3], rng[:, 0:1], F2_SPAN, None, ALU.is_le).then_inc(rng_step, 1)
            dve.wait_ge(rng_step, 3)
            dve.scalar_tensor_tensor(out=rng[:, 3:4], in0=rng[:, 1:2], scalar=F_ABS, in1=rng[:, 2:3],
                                     op0=ALU.is_le, op1=ALU.mult).then_inc(rng_step, 1)
            dve.wait_ge(rng_step, 4)
            dve.scalar_tensor_tensor(out=rng[:, 0:1], in0=gst[:, 3:4], scalar=X_MAX, in1=rng[:, 3:4],
                                     op0=ALU.is_le, op1=ALU.mult).then_inc(rng_step, 1)
            dve.wait_ge(rng_step, 5)
            dve.scalar_tensor_tensor(out=flag[:, :], in0=gst[:, 3:4], scalar=X_MIN, in1=rng[:, 0:1],
                                     op0=ALU.is_ge, op1=ALU.mult).then_inc(flag_ready, 1)
            go = fast(dve)
            with dve.If(go):
                f1n, f2max = f12[:, :, 0], gst[:, 0:1]
                dve.tensor_scalar(gsum[:, :], f1n, f2max, None, ALU.add).then_inc(tab_step, 1)
                dve.wait_ge(tab_step, 1)
                dve.scalar_tensor_tensor(out=mrow[:, :], in0=gsum[:, :], scalar=NEG_SLOPE, in1=gsum[:, :],
                                         op0=ALU.mult, op1=ALU.max).then_inc(tab_step, 1)
                dve.wait_ge(tab_step, 2)
                dve.tensor_tensor(ea[:, 0, :], gsum[:, :], mrow[:, :], ALU.subtract)
                dve.scalar_tensor_tensor(out=ea[:, 1, :], in0=f1n, scalar=NEG_SLOPE, in1=mrow[:, :],
                                         op0=ALU.mult, op1=ALU.subtract).then_inc(ea_ready, 1)
                dve.wait_ge(exp_ready, 1)
                dve.tensor_scalar(p2[:, :].bitcast(I32), be[:, :].bitcast(I32), 0x7F800000, None,
                                  ALU.bitwise_and).then_inc(tab_step, 1)
                dve.wait_ge(tab_step, 3)
                dve.tensor_scalar(p2[:, :], p2[:, :], PAT_MIN, None, ALU.max).then_inc(tab_step, 1)
                dve.wait_ge(tab_step, 4)
                dve.tensor_copy(pat[:, :], p2[:, :], saturate=False)
                dve.reciprocal(rp[:, :], p2[:, :]).then_inc(tab_step, 1)
                dve.wait_ge(tab_step, 5)
                dve.scalar_tensor_tensor(out=cs[:, 0, :], in0=be[:, :], scalar=SCALE, in1=rp[:, :],
                                         op0=ALU.mult, op1=ALU.mult).then_inc(tab_step, 1)
                dve.wait_ge(exp_ready, 2)
                dve.tensor_scalar(cs[:, 1, :], de[:, :], SCALE, None, ALU.mult).then_inc(tab_step, 1)
                dve.wait_ge(tab_step, 7)
                dve.wait_ge(xl_in, 16 * A)
                xlv = xl.rearrange("p (n d) -> p n d", n=NK)

                def scale_x(i):
                    m, h = i // BCH, i % BCH
                    part = slice(h * CN, (h + 1) * CN)
                    if i >= 2:
                        dve.wait_ge(table_ready, i - 1)
                    dve.tensor_copy(ybuf[:, i % 2, :, D], cs[:, m, part])
                    dve.tensor_tensor(ybuf[:, i % 2, :, 0:D], xlv[:, part, :],
                                      cs[:, m, part, None].to_broadcast([P, CN, D]),
                                      ALU.mult).then_inc(y_ready, 1)

                def pair(u, q, s, h):
                    slot = h
                    for c in range(2):
                        dve.wait_ge(nat_in[c], 16 * A * (u + 1))
                        apart(dve)
                        dve.tensor_scalar(mnt[:, 0, c * NK * P:(c + 1) * NK * P].bitcast(FP8), nat[:, c, :], 0,
                                          None, ALU.is_gt, saturate=False).then_inc(cast_done, 1)
                    dve.wait_ge(cast_done, 2 * u + 2)
                    for c in range(2):
                        dve.transpose(mt_w[:, :, c * P:(c + 1) * P].rearrange("p b (g s) -> p g b s", g=G),
                                      mn_w[:, c * NK * SQ:(c + 1) * NK * SQ].rearrange("p (g b r) -> p g b r", g=G, b=NB)
                                      ).then_inc(turn_done, 1)
                    dve.wait_ge(turn_done, 2 * u + 2)
                    dve.wait_ge(sign_ready, NB * (q + 1))
                    if not (isinstance(u, int) and u < 2):
                        dve.wait_ge(sums_made, 2 * u - 2)
                    sw = sgn_w[s][:, :, h * PW:(h + 1) * PW]
                    for b in range(NB):
                        ins = dve.scalar_tensor_tensor(out=mask_w[slot][0][:, b, :], in0=sw[:, b, :],
                                                       scalar=pat[:, :].bitcast(U32)[:, b:b + 1],
                                                       in1=mt_w[:, b, :], op0=ALU.bitwise_and,
                                                       op1=ALU.bitwise_and)
                    ins.then_inc(plus_ready, 1)
                    dve.scalar_tensor_tensor(out=mask_w[slot][1][:, :, :], in0=sw, scalar=0xFFFFFFFF,
                                             in1=mt_w[:, :, :], op0=ALU.bitwise_xor,
                                             op1=ALU.bitwise_and).then_inc(minus_ready, 1)

                def weights(q, s):
                    dve.wait_ge(sums_added, q + 1)
                    dve.tensor_scalar(iso[:, :], ntot[:, :, D], 0.0, None, ALU.is_equal).then_inc(rec_step, 1)
                    dve.wait_ge(rec_step, 3 * q + 1)
                    dve.scalar_tensor_tensor(out=den[:, :], in0=iso[:, :], scalar=float(N), in1=ntot[:, :, D],
                                             op0=ALU.mult, op1=ALU.add).then_inc(rec_step, 1)
                    dve.wait_ge(rec_step, 3 * q + 2)
                    dve.reciprocal(rec[:, :], den[:, :]).then_inc(rec_step, 1)

                def moments(q, s):
                    dve.wait_ge(y_done, q + 1)
                    for c in range(QT):
                        dve.bn_stats(bns[:, s, c, :], ybt[:, s, c, :]).then_inc(bn_step, 1)
                    dve.wait_ge(bn_step, QT * (q + 1))
                    apart(dve)
                    for c in range(QT):
                        ins = dve.bn_aggr(mv[:, s, c, :], bns[:, s, c, :])
                    ins.then_inc(mv_ready, 1)

                def normalise(q, s):
                    dve.wait_ge(rstd_ready, q + 1)
                    for c in range(QT):
                        ins = dve.tensor_scalar(ybt[:, s, c, :], ybt[:, s, c, :], mv[:, s, c, 0:1],
                                                rstd[:, s, c:c + 1], ALU.subtract, ALU.mult)
                    ins.then_inc(out_ready, 1)

                def quad(q, s, old=True):
                    pair(2 * q, q, s, 0)
                    if old:
                        weights(q - 2, s)
                    pair(2 * q + 1, q, s, 1)
                    if old:
                        moments(q - 2, s)
                        normalise(q - 2, s)

                for i in range(2 * BCH):
                    scale_x(i)
                dve.wait_ge(y_ready, 2 * BCH)
                quad(0, 0, old=False)
                quad(1, 1, old=False)
                with dve.Fori(1, NQ // 2) as turn:
                    quad(2 * turn, 0)
                    quad(2 * turn + 1, 1)
                for q in (NQ - 2, NQ - 1):
                    weights(q, q % 2)
                    moments(q, q % 2)
                    normalise(q, q % 2)
            with dve.Else():
                f2r = bt[:, 0].bitcast(F32)[:, 0:N]
                z = bt[:, 1].bitcast(F32)[:, 0:N]
                s_nat = sgn[:, 0].bitcast(F32)
                pT = sgn[:, 1].bitcast(F32)
                for g in range(NXG):
                    dve.wait_ge(g_f2_made, g + 1)
                    dve.tensor_scalar(f2r[:, g * 512:(g + 1) * 512], ps[:, g % 2, :], b12[:, 1:2], None,
                                      ALU.add).then_inc(g_f2_ready, 1)
                dve.wait_ge(g_f2_ready, NXG)
                STEPS = 7
                with dve.Fori(0, NT) as t:
                    dve.tensor_scalar(z, f2r, f12[:, bass.ds(t, 1), 0], None, ALU.add).then_inc(g_step, 1)
                    dve.wait_ge(g_step, STEPS * t + 1)
                    dve.scalar_tensor_tensor(out=z, in0=z, scalar=NEG_SLOPE, in1=z, op0=ALU.mult,
                                             op1=ALU.max).then_inc(g_step, 1)
                    dve.wait_ge(g_adj_in, 16 * (t + 1))
                    dve.tensor_scalar(s_nat, nat[:, 0, :], 0, 1.0, ALU.is_gt, ALU.subtract).then_inc(g_step, 1)
                    dve.wait_ge(g_step, STEPS * t + 3)
                    dve.scalar_tensor_tensor(out=s_nat, in0=s_nat, scalar=NEG_INF, in1=z, op0=ALU.mult,
                                             op1=ALU.add).then_inc(g_step, 1)
                    dve.wait_ge(g_step, STEPS * t + 4)
                    dve.tensor_reduce(gnmax[:, 0:1], s_nat, AX_X, ALU.max, negate=True).then_inc(g_max_ready, 1)
                    for g in range(NXG):
                        dve.wait_ge(g_turned, NXG * t + g + 1)
                        dve.tensor_copy(pT[:, g * 512:(g + 1) * 512], ps[:, g % 2, :]).then_inc(g_pt_ready, 1)
                    dve.reciprocal(rec[:, 0:1], gden[:, 0:1]).then_inc(g_step, 1)
                    dve.wait_ge(g_step, STEPS * t + 5)
                    dve.wait_ge(g_sum_made, t + 1)
                    dve.scalar_tensor_tensor(out=ybt[:, 0, 0, :], in0=ps[:, 2, 0:D], scalar=rec[:, 0:1],
                                             in1=xn[:, bass.ds(t, 1), :].rearrange("p o d -> p (o d)"),
                                             op0=ALU.mult, op1=ALU.add).then_inc(g_step, 1)
                    dve.wait_ge(g_step, STEPS * t + 6)
                    dve.bn_stats(bns[:, 0, 0, :], ybt[:, 0, 0, :]).then_inc(g_step, 1)
                    dve.wait_ge(g_step, STEPS * t + 7)
                    apart(dve)
                    dve.bn_aggr(mv[:, 0, 0, :], bns[:, 0, 0, :]).then_inc(mv_ready, 1)
                    dve.wait_ge(g_rstd, t + 1)
                    dve.wait_ge(g_stored, 16 * t)
                    dve.tensor_scalar(ybt[:, 1, 0, :], ybt[:, 0, 0, :], mv[:, 0, 0, 0:1], rstd[:, 0, 0:1],
                                      ALU.subtract, ALU.mult).then_inc(g_out_ready, 1)
            dve.nop()

        @block.tensor
        def _(pe):
            pe.wait_ge(weights_in, 80)
            pe.wait_ge(wbc_ready, 2)
            pe.matmul(ps[:, 4, 0:P], wsb[:, :], wbc[:, 0, :], start=True, stop=True)
            pe.matmul(ps[:, 4, P:2 * P], wsb[:, :], wbc[:, 1, :], start=True, stop=True)
            pe.matmul(ps[:, 4, 2 * P:2 * P + 2], wsb[:, :], w12[:, :], start=True, stop=True).then_inc(v_made, 1)

            def spread_f1(g):
                pe.wait_ge(xT_ready, g + 1)
                if g >= 2:
                    pe.wait_ge(f1b_ready, g - 1)
                pe.matmul(ps[:, 2 + g % 2, :], vsb[:, 0:P], xT[:, g * 512:(g + 1) * 512],
                          start=True, stop=True).then_inc(f1_made, 1)

            for g in range(NXG):
                pe.wait_ge(xn_in[g * XG // (NT // 4)], 16)
                if g >= 2:
                    pe.wait_ge(xT_ready, g - 1)
                for c in range(XG):
                    ins = pe.transpose(ps[:, g % 2, c * P:(c + 1) * P], xn[:, g * XG + c, :], ident[:, :])
                ins.then_inc(x_turned, 1)
                if g == 0:
                    pe.wait_ge(vsb_ready, 1)
                else:
                    spread_f1(g - 1)
            spread_f1(NXG - 1)
            v12 = vsb[:, 2 * P:2 * P + 2]
            for t in range(NT):
                pe.matmul(ps[:, 5, 2 * t:2 * t + 2], xT[:, t * P:(t + 1) * P], v12, start=True, stop=True)
            pe.wait_ge(xTp_ready, NXG)
            for n in range(NK):
                ins = pe.matmul(ps[:, 6, n:n + 1], xTp[:, n * P:(n + 1) * P], v12[:, 1:2], start=True, stop=True)
            ins.then_inc(f_made, 1)
            pe.wait_ge(stat_ready, 1)
            pe.transpose(ps[0:4, 7, 0:P], stat[:, :], ident[:, :]).then_inc(stat_turned, 1)
            pe.wait_ge(diag_ready, 1)
            pe.matmul(ps[:, 7, 256:260], ones[0:4, :], stdiag[:, :], start=True, stop=True).then_inc(gst_made, 1)
            go = fast(pe)
            with pe.If(go):
                for t in range(NT):
                    ins = pe.matmul(ps[:, 7, 0:D], ones[:, :], xn[:, t, :], start=(t == 0), stop=(t == NT - 1))
                ins.then_inc(xsum_made, 1)

                def pair(u, slot, first=False):
                    for c in range(2):
                        if not (isinstance(u, int) and u == 0):
                            pe.wait_ge(sums_out, 2 * u + c - 1)
                            apart(pe)
                        for m, ready in enumerate((plus_ready, minus_ready)):
                            if c == 0:
                                pe.wait_ge(ready, u + 1)
                                apart(pe)
                            for n in range(NK):
                                if first and c == 0 and n % CN == 0:
                                    pe.wait_ge(table_ready, m * BCH + n // CN + 1)
                                ins = pe.matmul(ps[:, 2 * c + m, 0:2 * DV],
                                                mask_f[slot][m][:, n // KB, n % KB, c * P:(c + 1) * P],
                                                btv[m][:, n, :], start=(n == 0), stop=(n == NK - 1))
                        ins.then_inc(sums_made, 1)

                pair(0, 0, first=True)
                pair(1, 1)
                with pe.Fori(1, NT // 4) as turn:
                    pair(2 * turn, 0)
                    pair(2 * turn + 1, 1)
            with pe.Else():
                for g in range(NXG):
                    if g >= 2:
                        pe.wait_ge(g_f2_ready, g - 1)
                    pe.matmul(ps[:, g % 2, :], vsb[:, P:2 * P], xT[:, g * 512:(g + 1) * 512],
                              start=True, stop=True).then_inc(g_f2_made, 1)
                pe.wait_ge(g_f2_ready, NXG)
                P_nat = sgn[:, 0].bitcast(F32)
                pT = sgn[:, 1].bitcast(F32)
                with pe.Fori(0, NT) as t:
                    pe.wait_ge(g_exp_ready, t + 1)
                    for g in range(NXG):
                        if g >= 2:
                            pe.wait_ge(g_pt_ready, NXG * t + g - 1)
                        for c in range(XG):
                            j = g * XG + c
                            ins = pe.transpose(ps[:, g % 2, c * P:(c + 1) * P], P_nat[:, j * P:(j + 1) * P],
                                               ident[:, :])
                        ins.then_inc(g_turned, 1)
                    pe.wait_ge(g_pt_ready, NXG * t + NXG)
                    for j in range(NT):
                        ins = pe.matmul(ps[:, 2, 0:D], pT[:, j * P:(j + 1) * P], xn[:, j, :],
                                        start=(j == 0), stop=(j == NT - 1))
                    ins.then_inc(g_sum_made, 1)
            pe.nop()


_INS = ["x", "adj", "L0_gnn_W", "L0_gnn_w1", "L0_gnn_b1", "L0_gnn_w2", "L0_gnn_b2"]


def kernel(**inputs):
    import numpy as np
    import concourse.bacc as bacc
    from concourse.bass_utils import run_bass_kernel_spmd

    nc = bacc.Bacc("TRN2", target_bir_lowering=False, num_devices=1)
    arrays, args = {}, []
    for name in _INS:
        a = np.ascontiguousarray(inputs[name])
        arrays[f"in_{name}"] = a
        args.append(nc.dram_tensor(f"in_{name}", a.shape, mybir.dt.from_np(a.dtype), kind="ExternalInput").ap())
    out = nc.dram_tensor("out", inputs["x"].shape, F32, kind="ExternalOutput").ap()
    gat_kernel(nc, *args, out)
    r = run_bass_kernel_spmd(nc, [arrays], core_ids=[0])
    return r.results[0]["out"]
```

```python
from contextlib import ExitStack

import concourse.bass as bass
from concourse import mybir

ALU = mybir.AluOpType
ACT = mybir.ActivationFunctionType
F32 = mybir.dt.float32
F16 = mybir.dt.float16
FP8 = mybir.dt.float8e5
I32 = mybir.dt.int32
U32 = mybir.dt.uint32
U8 = mybir.dt.uint8
I8 = mybir.dt.int8
AX_X = mybir.AxisListType.X

P = 128
SQ = 32
NEG_SLOPE = 0.01
NEG_INF = 1.0e9
EPS = 1.0e-5
SCALE = 1024.0
PAT_MIN = 2.0 ** -14

F2_SPAN = 17.0
F_ABS = 31.0
X_MAX = 30.0
X_MIN = 2.0 ** -6


def gat_kernel(nc, x, adj, W, w1, b1, w2, b2, out):
    N, D = x.shape
    NT = N // P
    QT = 4
    NQ = NT // QT
    A = P // SQ
    JA = N // A
    KB = 4
    NB = JA // (SQ * KB)
    NK = NB * KB
    G = P // SQ
    DV = D + 1
    XG = KB
    NXG = NK // XG
    BCH = 4
    CN = NK // BCH
    PW = 2 * P
    QW = QT * P

    adj_v = adj.rearrange("(t g s) (a c) -> t a s g c", g=G, s=SQ, a=A)
    x_rows = x.rearrange("(t p) d -> p t d", p=P)
    x_cols = x.rearrange("(a b r k) d -> a r b (k d)", a=A, b=NB, r=SQ)
    out_q = out.rearrange("(q c p) d -> q p c d", c=QT, p=P)
    adj_t = adj.rearrange("(t p) j -> t p j", p=P)
    out_t = out.rearrange("(t p) d -> t p d", p=P)

    with ExitStack() as ctx:
        def sb(name, shape, dt):
            return ctx.enter_context(nc.sbuf_tensor(name, shape, dt))

        def sem(name):
            return ctx.enter_context(nc.semaphore(name))

        xn = sb("xn", [P, NT, D], F32)
        f1b = sb("f1b", [P, N], F32)
        f1n = sb("f1n", [P, NT], F32)
        f2l = sb("f2l", [P, NK], F32)
        nf2l = sb("nf2l", [P, NK], F32)
        wsb = sb("wsb", [P, D], F32)
        w12 = sb("w12", [P, 2], F32)
        b12 = sb("b12", [P, 2], F32)
        wbc = sb("wbc", [P, 2, P], F32)
        vsb = sb("vsb", [P, 3, P], F32)
        ident = sb("ident", [P, P], F32)
        ones = sb("ones", [P, P], F32)
        xmax = sb("xmax", [P, BCH], F32)
        f2raw = sb("f2raw", [P, NK], F32)
        stat = sb("stat", [P, 4], F32)
        stmax = sb("stmax", [2, 2], F32)
        stdiag = sb("stdiag", [2, 4], F32)
        gst = sb("gst", [P, 4], F32)
        rng = sb("rng", [P, 4], F32)
        flag = sb("flag", [P, 1], I32)
        nF2 = sb("nF2", [P, 1], F32)

        nat = sb("nat", [P, 2, G * JA], I32)
        masks = sb("masks", [P, 2, 2, NK * PW], U8)
        mnt = sb("mnt", [P, 2, NK * PW], U8)
        sgn = sb("sgn", [P, 2, NK * QW], I8)
        bt = sb("bt", [P, 2, NK * 2 * DV], F16)
        post = sb("post", [P, 2, 2, QT, 2 * DV], F32)

        xl = masks[:, 1].rearrange("p s n -> p (s n)").bitcast(F32)
        xT = masks[:, 0].rearrange("p s n -> p (s n)").bitcast(F32)
        xv = sgn[:, 1].bitcast(F32)
        ybuf = post.rearrange("p s m c d -> p (s m c d)").rearrange("p (h n d) -> p h n d", h=BCH, n=CN)
        mn_w = mnt[:, 0].bitcast(U32)
        mt_w = mnt[:, 1].bitcast(U32).rearrange("p (b i) -> p b i", b=NB)
        sgn_w = [sgn[:, s].bitcast(U32).rearrange("p (b i) -> p b i", b=NB) for s in range(2)]
        sgn_b = [sgn[:, s].rearrange("p (b i k) -> p b i k", b=NB, k=KB) for s in range(2)]
        mask_w = [[masks[:, s, m].bitcast(U32).rearrange("p (b i) -> p b i", b=NB) for m in range(2)]
                  for s in range(2)]
        mask_f = [[masks[:, s, m].bitcast(FP8).rearrange("p (b i k) -> p b k i", b=NB, k=KB)
                   for m in range(2)] for s in range(2)]
        btv = [bt[:, m].rearrange("p (n d) -> p n d", n=NK) for m in range(2)]

        be = sb("be", [P, NK], F32)
        de = sb("de", [P, NK], F32)
        p2 = sb("p2", [P, NK], F32)
        rp = sb("rp", [P, NK], F32)
        cs = sb("cs", [P, 2, NK], F32)
        pat = sb("pat", [P, NK], FP8)
        gsum = sb("gsum", [P, NT], F32)
        mrow = sb("mrow", [P, NT], F32)
        ea = sb("ea", [P, 2, NT], F32)
        ac = sb("ac", [P, 2, NT], F32)
        xsum = sb("xsum", [P, DV], F32)
        ntot = sb("ntot", [P, QT, DV], F32)
        iso = sb("iso", [P, QT], F32)
        den = sb("den", [P, QT], F32)
        rec = sb("rec", [P, QT], F32)
        isox = sb("isox", [P, QT, DV], F32)
        ybt = sb("ybt", [P, 2, QT, D], F32)
        bns = sb("bns", [P, 2, QT, 6], F32)
        mv = sb("mv", [P, 2, QT, 2], F32)
        vpe = sb("vpe", [P, QT], F32)
        mhalf = sb("mhalf", [P, QT], F32)
        rstd = sb("rstd", [P, 2, QT], F32)

        own = sb("own", [P, 3, QT], F32)
        iso_l, rec_l, vpe_l = own[:, 0], own[:, 1], own[:, 2]
        gnmax = iso[:, 0:1]
        gden = den[:, 0:1]

        ps = ctx.enter_context(nc.psum_tensor("ps", [P, 8, 512], F32))

        w_in = sem("w_in")
        w12_in = sem("w12_in")
        b12_in = sem("b12_in")
        xl_in = [sem(f"xl_in{i}") for i in range(BCH)]
        xn_in = sem("xn_in")
        ident_zero = sem("ident_zero")
        consts_ready = sem("consts_ready")
        wbc_ready = sem("wbc_ready")
        v_made = sem("v_made")
        vsb_ready = sem("vsb_ready")
        xv_dve = sem("xv_dve")
        xv_pool = sem("xv_pool")
        x_turned = sem("x_turned")
        xT_ready = [sem(f"xT_ready{i}") for i in range(2)]
        f1_made = sem("f1_made")
        f1b_ready = sem("f1b_ready")
        f1n_made = sem("f1n_made")
        f1n_ready = sem("f1n_ready")
        f2raw_ready = sem("f2raw_ready")
        f2l_ready = sem("f2l_ready")
        nf2l_ready = sem("nf2l_ready")
        xmax_ready = sem("xmax_ready")
        stat_ready = sem("stat_ready")
        stat_turned = sem("stat_turned")
        stmax_ready = sem("stmax_ready")
        diag_ready = sem("diag_ready")
        gst_made = sem("gst_made")
        gst_ready = sem("gst_ready")
        nF2_ready = sem("nF2_ready")
        rng_step = sem("rng_step")
        nat_in = [sem(f"nat_in{i}") for i in range(2)]
        exp_ready = sem("exp_ready")
        tab_step = sem("tab_step")
        rows_ready = sem("rows_ready")
        ea_ready = sem("ea_ready")
        y_ready = sem("y_ready")
        hi_ready = sem("hi_ready")
        table_ready = sem("table_ready")
        xsum_made = sem("xsum_made")
        xsum_ready = sem("xsum_ready")
        sign_ready = sem("sign_ready")
        cast_done = sem("cast_done")
        turn_done = sem("turn_done")
        first_plus = sem("first_plus")
        plus_ready = sem("plus_ready")
        minus_ready = sem("minus_ready")
        sums_made = sem("sums_made")
        sums_out = sem("sums_out")
        sums_added = sem("sums_added")
        pool_step = sem("pool_step")
        rec_step = sem("rec_step")
        y_done = sem("y_done")
        bn_step = sem("bn_step")
        mv_ready = sem("mv_ready")
        rstd_ready = sem("rstd_ready")
        out_ready = sem("out_ready")
        last_step = sem("last_step")
        last_ready = sem("last_ready")
        last_var_ready = sem("last_var_ready")
        last_rstd_ready = sem("last_rstd_ready")
        last_stored = sem("last_stored")
        out_stored = [sem(f"out_stored{i}") for i in range(2)]
        g_adj_in = sem("g_adj_in")
        g_xT_made = sem("g_xT_made")
        g_xT_ready = sem("g_xT_ready")
        g_f2_made = sem("g_f2_made")
        g_f2_ready = sem("g_f2_ready")
        g_step = sem("g_step")
        g_max_ready = sem("g_max_ready")
        g_exp_ready = sem("g_exp_ready")
        g_turned = sem("g_turned")
        g_pt_ready = sem("g_pt_ready")
        g_sum_made = sem("g_sum_made")
        g_out_ready = sem("g_out_ready")
        g_rstd = sem("g_rstd")
        g_stored = sem("g_stored")
        flag_ready = sem("flag_ready")

        steps_begun = {e.engine: sem(f"steps_begun_{n}") for n, e in
                       (("pe", nc.tensor), ("dve", nc.vector), ("pool", nc.gpsimd))}

        def xl_chunk(h):
            return xl.rearrange("p (n d) -> p n d", n=NK)[:, h * CN:(h + 1) * CN, :]

        def xv_chunk(h):
            return xv.rearrange("p (n d) -> p n d", n=NK)[:, h * CN:(h + 1) * CN, :]

        v2_rows = vsb[:, 2:3, :].to_broadcast([P, CN, D])

        block = ctx.enter_context(nc.Block())

        def fast(eng):
            eng.wait_ge(flag_ready, 1)
            return eng.value_load(flag[0:1, 0:1], min_val=0, max_val=1)

        def apart(eng):
            eng.sem_inc(steps_begun[eng.engine], 1)

        @block.sync
        def _(sp):
            sp.dma_start(wsb[:, :], W).then_inc(w_in, 16)
            for h in range(BCH):
                two = slice(h * NB // BCH, (h + 1) * NB // BCH)
                for a in range(A):
                    sp.dma_start(xl[a * SQ:(a + 1) * SQ, :].rearrange("r (b n) -> r b n", b=NB)[:, two],
                                 x_cols[a][:, two]).then_inc(xl_in[h], 16)

            def load_adj(t, slot):
                for a in range(A):
                    dst = nat[a * SQ:(a + 1) * SQ, slot, :].rearrange("s (g c) -> s g c", g=G)
                    sp.dma_start(dst, adj_v[t, a]).then_inc(nat_in[slot], 16)

            load_adj(0, 0)
            load_adj(1, 1)
            sp.dma_start(xn[:, :, :], x_rows).then_inc(xn_in, 16)
            for t in (2, 3):
                sp.wait_ge(cast_done, t - 1)
                load_adj(t, t % 2)
            go = fast(sp)
            with sp.If(go):
                def load_quad(q):
                    for c in range(QT):
                        sp.wait_ge(cast_done, QT * q + c - 1)
                        load_adj(QT * q + c, c % 2)

                def store(q, s):
                    sp.wait_ge(out_ready, q + 1)
                    sp.dma_start(out_q[q], ybt[:, s]).then_inc(out_stored[s], 16)

                load_quad(1)
                load_quad(2)
                load_quad(3)
                store(0, 0)
                with sp.Fori(2, NQ // 2) as turn:
                    load_quad(2 * turn)
                    store(2 * turn - 3, 1)
                    load_quad(2 * turn + 1)
                    store(2 * turn - 2, 0)
                store(NQ - 3, 1)
                store(NQ - 2, 0)
                for c in range(QT):
                    sp.wait_ge(last_ready, c + 1)
                    sp.dma_start(out_q[NQ - 1][:, c], ybt[:, 1, c]).then_inc(last_stored, 16)
                for s in range(2):
                    sp.wait_ge(out_stored[s], 16 * (NQ // 2 - s))
                sp.wait_ge(last_stored, 16 * QT)
            with sp.Else():
                def load_rows(t):
                    sp.dma_start(nat[:, 0, :], adj_t[t]).then_inc(g_adj_in, 16)

                def store_rows(t):
                    sp.wait_ge(g_out_ready, t + 1)
                    sp.dma_start(out_t[t], ybt[:, 1, 0, :]).then_inc(g_stored, 16)

                for s in range(2):
                    sp.wait_ge(nat_in[s], 2 * 16 * A)
                load_rows(0)
                with sp.Fori(1, NT) as t:
                    sp.wait_ge(g_max_ready, t)
                    load_rows(t)
                    store_rows(t - 1)
                store_rows(NT - 1)
                sp.wait_ge(g_stored, 16 * NT)
            sp.nop()

        @block.gpsimd
        def _(pool):
            pool.memset(ident[:, :], 0.0).then_inc(ident_zero, 1)
            pool.memset(ones[:, :], 1.0)
            pool.memset(mhalf[:, :], -0.5)
            pool.memset(xsum[:, D:DV], float(N))
            pool.wait_ge(ident_zero, 1)
            pool.affine_select(out=ident[:, :], in_=ident[:, :], compare_op=ALU.not_equal, fill=1.0,
                               base=0, pattern=[[-1, P]], channel_multiplier=1).then_inc(consts_ready, 1)
            pool.wait_ge(vsb_ready, 1)
            for h in (1, 3):
                pool.wait_ge(xl_in[h], 16 * A)
                pool.tensor_tensor(xv_chunk(h), xl_chunk(h), v2_rows, ALU.mult).then_inc(xv_pool, 1)
            for i in range(2 * BCH):
                m, h = i // BCH, i % BCH
                part = slice(h * CN, (h + 1) * CN)
                pool.wait_ge(hi_ready, i + 1)
                pool.tensor_tensor(btv[m][:, part, DV:2 * DV], ybuf[:, h], btv[m][:, part, 0:DV],
                                   ALU.subtract).then_inc(table_ready, 1)
            go = fast(pool)
            with pool.If(go):
                PSTEPS = 6

                def quad(q, s):
                    pool.wait_ge(sums_out, QT * (q + 1))
                    pool.tensor_tensor(post[:, s, 0], post[:, s, 0], post[:, s, 1],
                                       ALU.add).then_inc(pool_step, 1)
                    pool.wait_ge(pool_step, PSTEPS * q + 1)
                    pool.tensor_tensor(ntot[:, :, :], post[:, s, 0, :, 0:DV], post[:, s, 0, :, DV:2 * DV],
                                       ALU.add).then_inc(sums_added, 1)
                    pool.wait_ge(rec_step, 3 * q + 3)
                    pool.wait_ge(xsum_ready, 1)
                    pool.tensor_tensor(isox[:, :, :], xsum[:, None, :].to_broadcast([P, QT, DV]),
                                       iso[:, :, None].to_broadcast([P, QT, DV]),
                                       ALU.mult).then_inc(pool_step, 1)
                    pool.wait_ge(pool_step, PSTEPS * q + 2)
                    pool.tensor_tensor(ntot[:, :, :], ntot[:, :, :], isox[:, :, :], ALU.add).then_inc(pool_step, 1)
                    pool.wait_ge(pool_step, PSTEPS * q + 3)
                    if not isinstance(q, int):
                        pool.wait_ge(out_stored[s], 8 * (q - s))
                    pool.tensor_tensor(ybt[:, s], ntot[:, :, 0:D],
                                       rec[:, :, None].to_broadcast([P, QT, D]),
                                       ALU.mult).then_inc(pool_step, 1)
                    pool.wait_ge(pool_step, PSTEPS * q + 4)
                    pool.wait_ge(xn_in, 16)
                    pool.tensor_tensor(ybt[:, s], ybt[:, s], xn[:, bass.ds(QT * q, QT), :],
                                       ALU.add).then_inc(y_done, 1)
                    pool.wait_ge(mv_ready, q + 1)
                    apart(pool)
                    pool.tensor_scalar(vpe[:, :], mv[:, s, :, 1], EPS, None, ALU.add).then_inc(pool_step, 1)
                    pool.wait_ge(pool_step, PSTEPS * q + 5)
                    pool.tensor_tensor(rstd[:, s], vpe[:, :], mhalf[:, :], ALU.pow).then_inc(rstd_ready, 1)
                    pool.tensor_tensor(ybt[:, s], ybt[:, s], mv[:, s, :, 0:1].to_broadcast([P, QT, D]),
                                       ALU.subtract).then_inc(pool_step, 1)
                    pool.wait_ge(pool_step, PSTEPS * q + 6)
                    pool.wait_ge(rstd_ready, q + 1)
                    pool.tensor_tensor(ybt[:, s], ybt[:, s], rstd[:, s, :, None].to_broadcast([P, QT, D]),
                                       ALU.mult).then_inc(out_ready, 1)

                quad(0, 0)
                quad(1, 1)
                with pool.Fori(1, NQ // 2 - 1) as turn:
                    quad(2 * turn, 0)
                    quad(2 * turn + 1, 1)
                quad(NQ - 2, 0)
                for c in range(QT):
                    pool.wait_ge(last_var_ready, c + 1)
                    pool.tensor_tensor(rstd[:, 1, c:c + 1], vpe_l[:, c:c + 1], mhalf[:, 0:1],
                                       ALU.pow).then_inc(last_rstd_ready, 1)
            with pool.Else():
                with pool.Fori(0, NT) as t:
                    pool.wait_ge(mv_ready, t + 1)
                    apart(pool)
                    pool.tensor_scalar(vpe[:, 0:1], mv[:, 0, 0, 1:2], EPS, None, ALU.add).then_inc(pool_step, 1)
                    pool.wait_ge(pool_step, t + 1)
                    pool.tensor_tensor(rstd[:, 0, 0:1], vpe[:, 0:1], mhalf[:, 0:1], ALU.pow).then_inc(g_rstd, 1)
            pool.nop()

        @block.scalar
        def _(act):
            act.dma_start(w12[:, 0:1], w1.rearrange("o h -> h o")).then_inc(w12_in, 16)
            act.dma_start(w12[:, 1:2], w2.rearrange("o h -> h o")).then_inc(w12_in, 16)
            act.dma_start(b12[:, 0:1], b1.partition_broadcast(P)).then_inc(b12_in, 16)
            act.dma_start(b12[:, 1:2], b2.partition_broadcast(P)).then_inc(b12_in, 16)

            def signs(q, s, b0, b1):
                for b in range(b0, b1):
                    for k in range(KB):
                        n = b * KB + k
                        ins = act.activation(sgn_b[s][:, b, :, k], f1b[:, bass.ds(q * QW, QW)], ACT.Sign,
                                             bias=nf2l[:, n:n + 1], scale=-1.0)
                    ins.then_inc(sign_ready, 1)

            def spread_out(b):
                act.wait_ge(f1_made, b + 1)
                act.activation(f1b[:, :].rearrange("p (a b r k) -> p b k a r", a=A, b=NB, r=SQ)[:, b],
                               ps[:, 4 + b % 2, :].rearrange("p (k a r) -> p k a r", k=KB, a=A), ACT.Identity,
                               bias=b12[:, 0:1]).then_inc(f1b_ready, 1)

            def split_x(i):
                m, h = i // BCH, i % BCH
                act.wait_ge(y_ready, i + 1)
                act.activation(btv[m][:, h * CN:(h + 1) * CN, 0:DV], ybuf[:, h], ACT.Copy).then_inc(hi_ready, 1)

            act.wait_ge(consts_ready, 1)
            act.activation(ac[:, 0, 0:1], ones[:, 0:1], ACT.Copy)
            for b in range(NXG):
                if b < NXG // 2:
                    act.wait_ge(x_turned, b + 1)
                    act.activation(xT[:, b * 512:(b + 1) * 512], ps[:, b % 4, :], ACT.Copy).then_inc(xT_ready[0], 1)
                if b == 1:
                    act.wait_ge(b12_in, 32)
                if b:
                    spread_out(b - 1)
                if b == QT:
                    act.wait_ge(f1b_ready, QT)
                    act.wait_ge(nf2l_ready, 1)
                    signs(0, 0, 0, 1)
                if b == QT + 1:
                    act.wait_ge(nF2_ready, 1)
                    act.activation(be[:, :], f2l[:, :], ACT.Exp, bias=nF2[:, 0:1]).then_inc(exp_ready, 1)
                    act.activation(de[:, :], f2l[:, :], ACT.Exp, scale=NEG_SLOPE).then_inc(exp_ready, 1)
            spread_out(NXG - 1)
            for i in range(2 * BCH):
                if i + 1 < NB:
                    signs(0, 0, i + 1, i + 2)
                split_x(i)
            go = fast(act)
            with act.If(go):
                def evacuate(q, s, c):
                    act.wait_ge(sums_made, QT * q + c + 1)
                    if c == 0 and not (isinstance(q, int) and q < 2):
                        act.wait_ge(sums_added, q - 1)
                    for m in range(2):
                        ins = act.activation(post[:, s, m, c, :], ps[:, 2 * (c % 2) + m, 0:2 * DV], ACT.Copy,
                                             scale=ac[:, m, bass.ds(QT * q + c, 1)])
                    ins.then_inc(sums_out, 1)

                def quad(q, s, more=True):
                    for c, (b0, b1) in enumerate(((0, 3), (3, 6), (6, 8), (8, 8))):
                        if more and b1 > b0:
                            if c == 0:
                                if not (isinstance(q, int) and q == 0):
                                    act.wait_ge(minus_ready, 2 * q)
                            signs(q + 1, 1 - s, b0, b1)
                        if isinstance(q, int) and q == 0 and c == 0:
                            act.wait_ge(ea_ready, 1)
                            act.activation(ac[:, :, :], ea[:, :, :], ACT.Exp).then_inc(rows_ready, 1)
                            act.wait_ge(rows_ready, 1)
                        evacuate(q, s, c)

                quad(0, 0)
                quad(1, 1)
                with act.Fori(1, NQ // 2 - 1) as turn:
                    quad(2 * turn, 0)
                    quad(2 * turn + 1, 1)
                quad(NQ - 2, 0)
                quad(NQ - 1, 1, more=False)

            with act.Else():
                P_nat = sgn[:, 0].bitcast(F32)
                with act.Fori(0, NT) as t:
                    act.wait_ge(g_max_ready, t + 1)
                    act.activation(P_nat, P_nat, ACT.Exp, bias=gnmax[:, 0:1],
                                   accum_out=gden[:, 0:1]).then_inc(g_exp_ready, 1)
            act.nop()

        @block.vector
        def _(dve):
            dve.wait_ge(w12_in, 32)
            dve.wait_ge(consts_ready, 1)
            for m in range(2):
                dve.tensor_scalar(wbc[:, m, :], ones[:, :], w12[:, m:m + 1], None, ALU.mult).then_inc(wbc_ready, 1)
            dve.wait_ge(v_made, 1)
            dve.tensor_copy(vsb[:, :, :].rearrange("p m n -> p (m n)"), ps[:, 6, 0:3 * P]).then_inc(vsb_ready, 1)
            def spread_stats(j):
                dve.wait_ge(stat_turned, j + 1)
                dve.tensor_reduce(stmax[:, j:j + 1], ps[0:2, 7, (1 + j) * P:(2 + j) * P], AX_X,
                                  ALU.max).then_inc(stmax_ready, 1)
                dve.wait_ge(stmax_ready, j + 1)
                dve.tensor_scalar(stdiag[:, 2 * j:2 * j + 2], ident[0:2, 0:2], stmax[:, j:j + 1], None,
                                  ALU.mult).then_inc(diag_ready, 1)
                dve.wait_ge(gst_made, j + 1)
                dve.tensor_copy(gst[:, 2 * j:2 * j + 2], ps[:, 7, 64 + 2 * j:66 + 2 * j]).then_inc(gst_ready, 1)
                dve.wait_ge(gst_ready, j + 1)

            def scale_x(i):
                m, h = i // BCH, i % BCH
                part = slice(h * CN, (h + 1) * CN)
                if i >= BCH:
                    dve.wait_ge(table_ready, i - BCH + 1)
                dve.tensor_copy(ybuf[:, h, :, D], cs[:, m, part])
                dve.tensor_tensor(ybuf[:, h, :, 0:D], xl_chunk(h),
                                  cs[:, m, part, None].to_broadcast([P, CN, D]),
                                  ALU.mult).then_inc(y_ready, 1)

            def edge_bytes(u, c):
                dve.wait_ge(nat_in[c], 16 * A * (u + 1))
                apart(dve)
                dve.tensor_scalar(mnt[:, 0, c * NK * P:(c + 1) * NK * P].bitcast(FP8), nat[:, c, :], 0,
                                  None, ALU.is_gt, saturate=False).then_inc(cast_done, 1)

            def turn_words(u, c):
                dve.wait_ge(cast_done, 2 * u + c + 1)
                dve.transpose(mt_w[:, :, c * P:(c + 1) * P].rearrange("p b (g s) -> p g b s", g=G),
                              mn_w[:, c * NK * SQ:(c + 1) * NK * SQ].rearrange("p (g b r) -> p g b r", g=G, b=NB)
                              ).then_inc(turn_done, 1)

            def plus(q, s, h, blocks):
                for b in blocks:
                    dve.wait_ge(sign_ready, NB * q + b + 1)
                    ins = dve.scalar_tensor_tensor(out=mask_w[h][0][:, b, :],
                                                   in0=sgn_w[s][:, b, h * PW:(h + 1) * PW],
                                                   scalar=pat[:, :].bitcast(U32)[:, b:b + 1],
                                                   in1=mt_w[:, b, :], op0=ALU.bitwise_and,
                                                   op1=ALU.bitwise_and)
                return ins

            def minus(s, h):
                dve.scalar_tensor_tensor(out=mask_w[h][1][:, :, :], in0=sgn_w[s][:, :, h * PW:(h + 1) * PW],
                                         scalar=0xFFFFFFFF, in1=mt_w[:, :, :], op0=ALU.bitwise_xor,
                                         op1=ALU.bitwise_and).then_inc(minus_ready, 1)

            def xv_product(h):
                dve.wait_ge(xl_in[h], 16 * A)
                dve.tensor_tensor(xv_chunk(h), xl_chunk(h), v2_rows, ALU.mult).then_inc(xv_dve, 1)

            def f2_sum(h):
                dve.wait_ge(xv_pool if h % 2 else xv_dve, h // 2 + 1)
                dve.tensor_reduce(f2raw[:, h * CN:(h + 1) * CN], xv_chunk(h), AX_X, ALU.add).then_inc(f2raw_ready, 1)

            def xT_out(b):
                dve.wait_ge(x_turned, b + 1)
                dve.tensor_copy(xT[:, b * 512:(b + 1) * 512], ps[:, b % 4, :]).then_inc(xT_ready[1], 1)

            def x_largest(h):
                dve.wait_ge(xl_in[h], 16 * A)
                dve.tensor_reduce(xmax[:, h:h + 1], xl_chunk(h).rearrange("p n d -> p (n d)"), AX_X, ALU.max,
                                  apply_absolute_value=True).then_inc(xmax_ready, 1)

            dve.wait_ge(vsb_ready, 1)
            xv_product(0)
            f2_sum(0)
            x_largest(0)
            xv_product(2)
            f2_sum(1)
            f2_sum(2)
            xT_out(4)
            f2_sum(3)
            dve.wait_ge(f2raw_ready, BCH)
            dve.wait_ge(b12_in, 32)
            dve.tensor_scalar(nf2l[:, :], f2raw[:, :], b12[:, 1:2], -1.0, ALU.add, ALU.mult).then_inc(nf2l_ready, 1)
            dve.tensor_scalar(f2l[:, :], f2raw[:, :], b12[:, 1:2], None, ALU.add).then_inc(f2l_ready, 1)
            dve.wait_ge(f2l_ready, 1)
            dve.tensor_reduce(stat[:, 0:1], f2l[:, :], AX_X, ALU.max)
            dve.tensor_reduce(stat[:, 1:2], f2l[:, :], AX_X, ALU.min, negate=True).then_inc(stat_ready, 1)
            xT_out(5)
            spread_stats(0)
            dve.tensor_scalar(nF2[:, :], gst[:, 0:1], -1.0, None, ALU.mult).then_inc(nF2_ready, 1)
            xT_out(6)
            xT_out(7)
            dve.wait_ge(exp_ready, 1)
            dve.tensor_scalar(p2[:, :].bitcast(I32), be[:, :].bitcast(I32), 0x7F800000, None,
                              ALU.bitwise_and).then_inc(tab_step, 1)
            dve.wait_ge(tab_step, 1)
            dve.tensor_scalar(p2[:, :], p2[:, :], PAT_MIN, None, ALU.max).then_inc(tab_step, 1)
            dve.wait_ge(tab_step, 2)
            dve.tensor_copy(pat[:, :], p2[:, :], saturate=False)
            dve.reciprocal(rp[:, :], p2[:, :]).then_inc(tab_step, 1)
            dve.wait_ge(tab_step, 3)
            dve.scalar_tensor_tensor(out=cs[:, 0, :], in0=be[:, :], scalar=SCALE, in1=rp[:, :],
                                     op0=ALU.mult, op1=ALU.mult).then_inc(tab_step, 1)
            dve.wait_ge(exp_ready, 2)
            dve.tensor_scalar(cs[:, 1, :], de[:, :], SCALE, None, ALU.mult).then_inc(tab_step, 1)
            dve.wait_ge(tab_step, 5)
            scale_x(0)
            edge_bytes(0, 0)
            scale_x(1)
            turn_words(0, 0)
            scale_x(2)
            edge_bytes(0, 1)
            turn_words(0, 1)
            scale_x(3)
            dve.wait_ge(turn_done, 2)
            dve.wait_ge(f1_made, NXG)
            for b in range(4):
                plus(0, 0, 0, [b]).then_inc(first_plus, 1)
            dve.wait_ge(f1n_made, 1)
            dve.tensor_copy(f1n[:, :], ps[:, 6, 0:NT]).then_inc(f1n_ready, 1)
            scale_x(4)
            x_largest(1)
            scale_x(5)
            x_largest(2)
            x_largest(3)
            dve.wait_ge(f1n_ready, 1)
            dve.tensor_reduce(stat[:, 2:3], f1n[:, :], AX_X, ALU.max, apply_absolute_value=True)
            dve.wait_ge(xmax_ready, BCH)
            dve.tensor_reduce(stat[:, 3:4], xmax[:, :], AX_X, ALU.max).then_inc(stat_ready, 1)
            for b in range(4, 6):
                plus(0, 0, 0, [b]).then_inc(first_plus, 1)
            scale_x(6)
            spread_stats(1)
            dve.tensor_tensor(rng[:, 0:1], gst[:, 0:1], gst[:, 1:2], ALU.add).then_inc(rng_step, 1)
            dve.scalar_tensor_tensor(out=rng[:, 1:2], in0=gst[:, 0:1], scalar=gst[:, 1:2], in1=gst[:, 2:3],
                                     op0=ALU.max, op1=ALU.add).then_inc(rng_step, 1)
            dve.wait_ge(rng_step, 2)
            dve.tensor_scalar(rng[:, 2:3], rng[:, 0:1], F2_SPAN, None, ALU.is_le).then_inc(rng_step, 1)
            dve.wait_ge(rng_step, 3)
            dve.scalar_tensor_tensor(out=rng[:, 3:4], in0=rng[:, 1:2], scalar=F_ABS, in1=rng[:, 2:3],
                                     op0=ALU.is_le, op1=ALU.mult).then_inc(rng_step, 1)
            dve.wait_ge(rng_step, 4)
            dve.scalar_tensor_tensor(out=rng[:, 0:1], in0=gst[:, 3:4], scalar=X_MAX, in1=rng[:, 3:4],
                                     op0=ALU.is_le, op1=ALU.mult).then_inc(rng_step, 1)
            dve.wait_ge(rng_step, 5)
            dve.scalar_tensor_tensor(out=flag[:, :], in0=gst[:, 3:4], scalar=X_MIN, in1=rng[:, 0:1],
                                     op0=ALU.is_ge, op1=ALU.mult).then_inc(flag_ready, 1)
            dve.tensor_scalar(gsum[:, :], f1n[:, :], gst[:, 0:1], None, ALU.add).then_inc(tab_step, 1)
            dve.wait_ge(tab_step, 6)
            dve.scalar_tensor_tensor(out=mrow[:, :], in0=gsum[:, :], scalar=NEG_SLOPE, in1=gsum[:, :],
                                     op0=ALU.mult, op1=ALU.max).then_inc(tab_step, 1)
            dve.wait_ge(tab_step, 7)
            dve.tensor_tensor(ea[:, 0, :], gsum[:, :], mrow[:, :], ALU.subtract)
            dve.scalar_tensor_tensor(out=ea[:, 1, :], in0=f1n[:, :], scalar=NEG_SLOPE, in1=mrow[:, :],
                                     op0=ALU.mult, op1=ALU.subtract).then_inc(ea_ready, 1)
            for b in range(6, NB):
                plus(0, 0, 0, [b]).then_inc(first_plus, 1)
            scale_x(7)
            minus(0, 0)
            dve.wait_ge(xsum_made, 1)
            dve.tensor_reduce(xsum[:, 0:D], ps[:, 4, :].rearrange("p (k d) -> p d k", d=D), AX_X,
                              ALU.add).then_inc(xsum_ready, 1)
            dve.wait_ge(y_ready, 2 * BCH)
            go = fast(dve)
            with dve.If(go):
                def pair(u, q, s, h, between=None):
                    edge_bytes(u, 0)
                    edge_bytes(u, 1)
                    turn_words(u, 0)
                    turn_words(u, 1)
                    if between:
                        between()
                    dve.wait_ge(turn_done, 2 * u + 2)
                    if not (isinstance(u, int) and u < 2):
                        dve.wait_ge(sums_made, 2 * u - 2)
                    plus(q, s, h, range(NB)).then_inc(plus_ready, 1)
                    minus(s, h)

                def weights(q, s):
                    dve.wait_ge(sums_added, q + 1)
                    dve.tensor_scalar(iso[:, :], ntot[:, :, D], 0.0, None, ALU.is_equal).then_inc(rec_step, 1)
                    dve.wait_ge(rec_step, 3 * q + 1)
                    dve.scalar_tensor_tensor(out=den[:, :], in0=iso[:, :], scalar=float(N), in1=ntot[:, :, D],
                                             op0=ALU.mult, op1=ALU.add).then_inc(rec_step, 1)
                    dve.wait_ge(rec_step, 3 * q + 2)
                    dve.reciprocal(rec[:, :], den[:, :]).then_inc(rec_step, 1)

                def moments(q, s):
                    dve.wait_ge(y_done, q + 1)
                    for c in range(QT):
                        dve.bn_stats(bns[:, s, c, :], ybt[:, s, c, :]).then_inc(bn_step, 1)
                    dve.wait_ge(bn_step, QT * (q + 1))
                    apart(dve)
                    for c in range(QT):
                        ins = dve.bn_aggr(mv[:, s, c, :], bns[:, s, c, :])
                    ins.then_inc(mv_ready, 1)

                def quad(q, s):
                    pair(2 * q, q, s, 0)
                    weights(q - 2, s)
                    pair(2 * q + 1, q, s, 1, between=lambda: moments(q - 2, s))

                pair(1, 0, 0, 1)
                pair(2, 1, 1, 0)
                pair(3, 1, 1, 1)
                with dve.Fori(1, NQ // 2) as turn:
                    quad(2 * turn, 0)
                    quad(2 * turn + 1, 1)

                q, s = NQ - 1, 1
                TAIL = 8

                def finish(c):
                    t = QT * q + c
                    done = TAIL * c

                    def step(ins):
                        nonlocal done
                        done += 1
                        ins.then_inc(last_step, 1)
                        dve.wait_ge(last_step, done)

                    dve.wait_ge(sums_out, t + 1)
                    step(dve.tensor_tensor(post[:, s, 0, c], post[:, s, 0, c], post[:, s, 1, c], ALU.add))
                    step(dve.tensor_tensor(post[:, s, 1, c, 0:DV], post[:, s, 0, c, 0:DV],
                                           post[:, s, 0, c, DV:2 * DV], ALU.add))
                    total = post[:, s, 1, c, 0:DV]
                    step(dve.tensor_scalar(iso_l[:, c:c + 1], total[:, D:DV], 0.0, None, ALU.is_equal))
                    step(dve.scalar_tensor_tensor(out=total, in0=xsum[:, :], scalar=iso_l[:, c:c + 1], in1=total,
                                                  op0=ALU.mult, op1=ALU.add))
                    step(dve.reciprocal(rec_l[:, c:c + 1], total[:, D:DV]))
                    if c == 0:
                        dve.wait_ge(out_stored[s], 16 * (NQ // 2 - 1))
                    step(dve.scalar_tensor_tensor(out=ybt[:, s, c], in0=total[:, 0:D], scalar=rec_l[:, c:c + 1],
                                                  in1=xn[:, t, :], op0=ALU.mult, op1=ALU.add))
                    step(dve.bn_stats(bns[:, s, c, :], ybt[:, s, c, :]))
                    step(dve.bn_aggr(mv[:, s, c, :], bns[:, s, c, :]))
                    dve.tensor_scalar(vpe_l[:, c:c + 1], mv[:, s, c, 1:2], EPS, None,
                                      ALU.add).then_inc(last_var_ready, 1)

                def normalise(c):
                    dve.wait_ge(last_rstd_ready, c + 1)
                    dve.tensor_scalar(ybt[:, s, c], ybt[:, s, c], mv[:, s, c, 0:1], rstd[:, s, c:c + 1],
                                      ALU.subtract, ALU.mult).then_inc(last_ready, 1)

                finish(0)
                weights(NQ - 2, 0)
                finish(1)
                moments(NQ - 2, 0)
                finish(2)
                for c in range(QT - 1):
                    normalise(c)
                finish(QT - 1)
                normalise(QT - 1)
            with dve.Else():
                f2r = bt[:, 0].bitcast(F32)[:, 0:N]
                z = bt[:, 1].bitcast(F32)[:, 0:N]
                s_nat = sgn[:, 0].bitcast(F32)
                pT = sgn[:, 1].bitcast(F32)
                dve.wait_ge(table_ready, 2 * BCH)
                for g in range(NXG):
                    dve.wait_ge(g_xT_made, g + 1)
                    dve.tensor_copy(xT[:, 0:512], ps[:, 3, :]).then_inc(g_xT_ready, 1)
                    dve.wait_ge(g_f2_made, g + 1)
                    dve.tensor_scalar(f2r[:, g * 512:(g + 1) * 512], ps[:, g % 2, :], b12[:, 1:2], None,
                                      ALU.add).then_inc(g_f2_ready, 1)
                dve.wait_ge(g_f2_ready, NXG)
                dve.wait_ge(xn_in, 16)
                STEPS = 7
                with dve.Fori(0, NT) as t:
                    dve.tensor_scalar(z, f2r, f1n[:, bass.ds(t, 1)], None, ALU.add).then_inc(g_step, 1)
                    dve.wait_ge(g_step, STEPS * t + 1)
                    dve.scalar_tensor_tensor(out=z, in0=z, scalar=NEG_SLOPE, in1=z, op0=ALU.mult,
                                             op1=ALU.max).then_inc(g_step, 1)
                    dve.wait_ge(g_adj_in, 16 * (t + 1))
                    dve.tensor_scalar(s_nat, nat[:, 0, :], 0, 1.0, ALU.is_gt, ALU.subtract).then_inc(g_step, 1)
                    dve.wait_ge(g_step, STEPS * t + 3)
                    dve.scalar_tensor_tensor(out=s_nat, in0=s_nat, scalar=NEG_INF, in1=z, op0=ALU.mult,
                                             op1=ALU.add).then_inc(g_step, 1)
                    dve.wait_ge(g_step, STEPS * t + 4)
                    dve.tensor_reduce(gnmax[:, 0:1], s_nat, AX_X, ALU.max, negate=True).then_inc(g_max_ready, 1)
                    for g in range(NXG):
                        dve.wait_ge(g_turned, NXG * t + g + 1)
                        dve.tensor_copy(pT[:, g * 512:(g + 1) * 512], ps[:, g % 2, :]).then_inc(g_pt_ready, 1)
                    dve.reciprocal(rec[:, 0:1], gden[:, 0:1]).then_inc(g_step, 1)
                    dve.wait_ge(g_step, STEPS * t + 5)
                    dve.wait_ge(g_sum_made, t + 1)
                    dve.scalar_tensor_tensor(out=ybt[:, 0, 0, :], in0=ps[:, 2, 0:D], scalar=rec[:, 0:1],
                                             in1=xn[:, bass.ds(t, 1), :].rearrange("p o d -> p (o d)"),
                                             op0=ALU.mult, op1=ALU.add).then_inc(g_step, 1)
                    dve.wait_ge(g_step, STEPS * t + 6)
                    dve.bn_stats(bns[:, 0, 0, :], ybt[:, 0, 0, :]).then_inc(g_step, 1)
                    dve.wait_ge(g_step, STEPS * t + 7)
                    apart(dve)
                    dve.bn_aggr(mv[:, 0, 0, :], bns[:, 0, 0, :]).then_inc(mv_ready, 1)
                    dve.wait_ge(g_rstd, t + 1)
                    dve.wait_ge(g_stored, 16 * t)
                    dve.tensor_scalar(ybt[:, 1, 0, :], ybt[:, 0, 0, :], mv[:, 0, 0, 0:1], rstd[:, 0, 0:1],
                                      ALU.subtract, ALU.mult).then_inc(g_out_ready, 1)
            dve.nop()

        @block.tensor
        def _(pe):
            pe.wait_ge(w_in, 16)
            for m in range(2):
                pe.wait_ge(wbc_ready, m + 1)
                pe.matmul(ps[:, 6, m * P:(m + 1) * P], wsb[:, :], wbc[:, m, :], start=True, stop=True)
            pe.matmul(ps[:, 6, 2 * P:3 * P], wbc[:, 1, :], wsb[:, :], start=True, stop=True).then_inc(v_made, 1)

            def spread_f1(b):
                half = b // (NXG // 2)
                pe.wait_ge(xT_ready[half], b - half * NXG // 2 + 1)
                if b >= 2:
                    pe.wait_ge(f1b_ready, b - 1)
                pe.matmul(ps[:, 4 + b % 2, :], vsb[:, 0, :], xT[:, b * 512:(b + 1) * 512],
                          start=True, stop=True).then_inc(f1_made, 1)

            def turn_stats(j):
                pe.wait_ge(stat_ready, j + 1)
                pe.transpose(ps[0:2, 7, (1 + j) * P:(2 + j) * P], stat[:, 2 * j:2 * j + 2],
                             ident[:, :]).then_inc(stat_turned, 1)

            def widen_stats(j):
                pe.wait_ge(diag_ready, j + 1)
                pe.matmul(ps[:, 7, 64 + 2 * j:66 + 2 * j], ones[0:2, :], stdiag[:, 2 * j:2 * j + 2],
                          start=True, stop=True).then_inc(gst_made, 1)

            for b in range(NXG):
                pe.wait_ge(xl_in[b * BCH // NB], 16 * A)
                if b == 0:
                    pe.wait_ge(consts_ready, 1)
                if b >= 4:
                    pe.wait_ge(xT_ready[0], b - 3)
                for k in range(KB):
                    n = b * KB + k
                    ins = pe.transpose(ps[:, b % 4, k * P:(k + 1) * P], xl[:, n * D:(n + 1) * D], ident[:, :])
                ins.then_inc(x_turned, 1)
                if b == 1:
                    pe.wait_ge(vsb_ready, 1)
                if b:
                    spread_f1(b - 1)
                if b == 5:
                    turn_stats(0)
                    widen_stats(0)
            spread_f1(NXG - 1)
            pe.wait_ge(f1b_ready, NXG)
            for t in range(NT):
                ins = pe.transpose(ps[:, 6, t:t + 1], f1b[0:1, t * P:(t + 1) * P], ident[0:1, 0:1])
            ins.then_inc(f1n_made, 1)

            def sum_rows(b):
                ins = pe.matmul(ps[:, 4, :], ones[:, :], xl[:, b * 512:(b + 1) * 512], start=(b == 0),
                                stop=(b == NXG - 1))
                if b == NXG - 1:
                    ins.then_inc(xsum_made, 1)

            for b in range(NXG):
                sum_rows(b)

            def edge_sums(slot, c, m, n, start, stop):
                return pe.matmul(ps[:, 2 * c + m, 0:2 * DV],
                                 mask_f[slot][m][:, n // KB, n % KB, c * P:(c + 1) * P],
                                 btv[m][:, n, :], start=start, stop=stop)

            for b in range(NB):
                pe.wait_ge(first_plus, b + 1)
                if b * KB % CN == 0:
                    pe.wait_ge(table_ready, b * KB // CN + 1)
                for c in range(2):
                    for k in range(KB):
                        n = b * KB + k
                        edge_sums(0, c, 0, n, n == 0, n == NK - 1)
                if b == 4:
                    turn_stats(1)
                if b == 5:
                    widen_stats(1)
            for c in range(2):
                pe.wait_ge(minus_ready, 1)
                for n in range(NK):
                    if n % CN == 0:
                        pe.wait_ge(table_ready, BCH + n // CN + 1)
                    ins = edge_sums(0, c, 1, n, n == 0, n == NK - 1)
                ins.then_inc(sums_made, 1)
            go = fast(pe)
            with pe.If(go):
                def pair(u, slot):
                    for c in range(2):
                        pe.wait_ge(sums_out, 2 * u + c - 1)
                        apart(pe)
                        for m, ready in enumerate((plus_ready, minus_ready)):
                            if c == 0:
                                pe.wait_ge(ready, u + 1 if m else u)
                                apart(pe)
                            for n in range(NK):
                                ins = edge_sums(slot, c, m, n, n == 0, n == NK - 1)
                        ins.then_inc(sums_made, 1)

                pair(1, 1)
                with pe.Fori(1, NT // 4) as turn:
                    pair(2 * turn, 0)
                    pair(2 * turn + 1, 1)
            with pe.Else():
                for g in range(NXG):
                    pe.wait_ge(xn_in, 16)
                    for c in range(XG):
                        ins = pe.transpose(ps[:, 3, c * P:(c + 1) * P], xn[:, g * XG + c, :], ident[:, :])
                    ins.then_inc(g_xT_made, 1)
                    pe.wait_ge(g_xT_ready, g + 1)
                    if g >= 2:
                        pe.wait_ge(g_f2_ready, g - 1)
                    pe.matmul(ps[:, g % 2, :], vsb[:, 1, :], xT[:, 0:512], start=True, stop=True).then_inc(g_f2_made, 1)
                pe.wait_ge(g_f2_ready, NXG)
                P_nat = sgn[:, 0].bitcast(F32)
                pT = sgn[:, 1].bitcast(F32)
                with pe.Fori(0, NT) as t:
                    pe.wait_ge(g_exp_ready, t + 1)
                    for g in range(NXG):
                        if g >= 2:
                            pe.wait_ge(g_pt_ready, NXG * t + g - 1)
                        for c in range(XG):
                            j = g * XG + c
                            ins = pe.transpose(ps[:, g % 2, c * P:(c + 1) * P], P_nat[:, j * P:(j + 1) * P],
                                               ident[:, :])
                        ins.then_inc(g_turned, 1)
                    pe.wait_ge(g_pt_ready, NXG * t + NXG)
                    for j in range(NT):
                        ins = pe.matmul(ps[:, 2, 0:D], pT[:, j * P:(j + 1) * P], xn[:, j, :],
                                        start=(j == 0), stop=(j == NT - 1))
                    ins.then_inc(g_sum_made, 1)
            pe.nop()


_INS = ["x", "adj", "L0_gnn_W", "L0_gnn_w1", "L0_gnn_b1", "L0_gnn_w2", "L0_gnn_b2"]


def kernel(**inputs):
    import numpy as np
    import concourse.bacc as bacc
    from concourse.bass_utils import run_bass_kernel_spmd

    nc = bacc.Bacc("TRN2", target_bir_lowering=False, num_devices=1)
    arrays, args = {}, []
    for name in _INS:
        a = np.ascontiguousarray(inputs[name])
        arrays[f"in_{name}"] = a
        args.append(nc.dram_tensor(f"in_{name}", a.shape, mybir.dt.from_np(a.dtype), kind="ExternalInput").ap())
    out = nc.dram_tensor("out", inputs["x"].shape, F32, kind="ExternalOutput").ap()
    gat_kernel(nc, *args, out)
    r = run_bass_kernel_spmd(nc, [arrays], core_ids=[0])
    return r.results[0]["out"]
```

```python
from contextlib import ExitStack

import concourse.bass as bass
from concourse import mybir

ALU = mybir.AluOpType
ACT = mybir.ActivationFunctionType
F32 = mybir.dt.float32
F16 = mybir.dt.float16
BF16 = mybir.dt.bfloat16
FP8 = mybir.dt.float8e5
I32 = mybir.dt.int32
U32 = mybir.dt.uint32
U8 = mybir.dt.uint8
I8 = mybir.dt.int8
AX_X = mybir.AxisListType.X

P = 128
SQ = 32
NEG_SLOPE = 0.01
NEG_INF = 1.0e9
EPS = 1.0e-5
PAT_MIN = 2.0 ** -14
SCALE = 64.0
EARLY = 3

F2_SPAN = 13.8
F_ABS = 31.0
X_MAX = 510.0
X_MIN = 0.25


def gat_kernel(nc, x, adj, W, w1, b1, w2, b2, out):
    N, D = x.shape
    NT = N // P
    QT = 4
    NQ = NT // QT
    A = P // SQ
    JA = N // A
    KB = 4
    NB = JA // (SQ * KB)
    NK = NB * KB
    G = P // SQ
    DV = D + 1
    XG = KB
    NXG = NK // XG
    BCH = 4
    CN = NK // BCH
    PW = 2 * P
    QW = QT * P

    adj_v = adj.rearrange("(t g s) (a c) -> t a s g c", g=G, s=SQ, a=A)
    x_rows = x.rearrange("(t p) d -> p t d", p=P)
    x_cols = x.rearrange("(a b r k) d -> a r b (k d)", a=A, b=NB, r=SQ)
    out_q = out.rearrange("(q c p) d -> q p c d", c=QT, p=P)
    adj_t = adj.rearrange("(t p) j -> t p j", p=P)
    out_t = out.rearrange("(t p) d -> t p d", p=P)

    with ExitStack() as ctx:
        def sb(name, shape, dt):
            return ctx.enter_context(nc.sbuf_tensor(name, shape, dt))

        def sem(name):
            return ctx.enter_context(nc.semaphore(name))

        xn = sb("xn", [P, NT, D], F32)
        f1b = sb("f1b", [P, N], F32)
        f1n = sb("f1n", [P, NT], F32)
        f2l = sb("f2l", [P, NK], F32)
        nf2l = sb("nf2l", [P, NK], F32)
        wsb = sb("wsb", [P, D], F32)
        w12 = sb("w12", [P, 2], F32)
        b12 = sb("b12", [P, 2], F32)
        wbc = sb("wbc", [P, 2, P], F32)
        vsb = sb("vsb", [P, 3, P], F32)
        ident = sb("ident", [P, P], F32)
        ones = sb("ones", [P, P], F32)
        f2raw = sb("f2raw", [P, NK], F32)
        stat = sb("stat", [P, 3], F32)
        stmax = sb("stmax", [2, 2], F32)
        stdiag = sb("stdiag", [2, 3], F32)
        gst = sb("gst", [P, 4], F32)
        rng = sb("rng", [P, 4], F32)
        flag = sb("flag", [P, 1], I32)
        nF2 = sb("nF2", [P, 1], F32)

        nat = sb("nat", [P, 2, G * JA], I32)
        masks = sb("masks", [P, 2, 2, NK * PW], U8)
        mnt = sb("mnt", [P, 2, NK * PW], U8)
        sgn = sb("sgn", [P, 2, NK * QW], I8)
        bt = sb("bt", [P, 2, NK * 2 * DV], F16)
        post = sb("post", [P, 2, 2, QT, 2 * DV], F32)

        xl = masks[:, 1].rearrange("p s n -> p (s n)").bitcast(F32)
        xT = masks[:, 0].rearrange("p s n -> p (s n)").bitcast(F32)
        xv = sgn[:, 1].bitcast(F32)
        x2 = sgn[:, 1].bitcast(BF16).rearrange("p (h n) -> p h n", h=BCH)[:, :, 0:CN * D]
        ybuf = post.rearrange("p s m c d -> p (s m c d)").rearrange("p (h n d) -> p h n d", h=BCH, n=CN)
        mn_w = mnt[:, 0].bitcast(U32)
        mt_w = mnt[:, 1].bitcast(U32).rearrange("p (b i) -> p b i", b=NB)
        sgn_w = [sgn[:, s].bitcast(U32).rearrange("p (b i) -> p b i", b=NB) for s in range(2)]
        sgn_b = [sgn[:, s].rearrange("p (b i k) -> p b i k", b=NB, k=KB) for s in range(2)]
        mask_w = [[masks[:, s, m].bitcast(U32).rearrange("p (b i) -> p b i", b=NB) for m in range(2)]
                  for s in range(2)]
        mask_f = [[masks[:, s, m].bitcast(FP8).rearrange("p (b i k) -> p b k i", b=NB, k=KB)
                   for m in range(2)] for s in range(2)]
        btv = [bt[:, m].rearrange("p (n d) -> p n d", n=NK) for m in range(2)]

        be = sb("be", [P, NK], F32)
        de = sb("de", [P, NK], F32)
        p2 = sb("p2", [P, NK], F32)
        rp = sb("rp", [P, NK], F32)
        cs = sb("cs", [P, 2, NK], F32)
        pat = sb("pat", [P, NK], FP8)
        gsum = sb("gsum", [P, NT], F32)
        mrow = sb("mrow", [P, NT], F32)
        ea = sb("ea", [P, 2, NT], F32)
        ac = sb("ac", [P, 2, NT], F32)
        xsum = sb("xsum", [P, DV], F32)
        ntot = sb("ntot", [P, QT, DV], F32)
        iso = sb("iso", [P, QT], F32)
        den = sb("den", [P, QT], F32)
        rec = sb("rec", [P, QT], F32)
        isox = sb("isox", [P, QT, DV], F32)
        ybt = sb("ybt", [P, 2, QT, D], F32)
        bns = sb("bns", [P, 2, QT, 6], F32)
        mv = sb("mv", [P, 2, QT, 2], F32)
        vpe = sb("vpe", [P, QT], F32)
        mhalf = sb("mhalf", [P, QT], F32)
        rstd = sb("rstd", [P, 2, QT], F32)
        nmr = sb("nmr", [P, 2, QT], F32)

        own = sb("own", [P, 4, QT], F32)
        iso_l, rec_l, vpe_l, rstd_l = (own[:, i] for i in range(4))
        gnmax = iso[:, 0:1]
        gden = den[:, 0:1]

        ps = ctx.enter_context(nc.psum_tensor("ps", [P, 8, 512], F32))

        w_in = sem("w_in")
        w12_in = sem("w12_in")
        b12_in = sem("b12_in")
        xl_in = [sem(f"xl_in{i}") for i in range(BCH)]
        xn_in = sem("xn_in")
        ident_zero = sem("ident_zero")
        consts_ready = sem("consts_ready")
        wbc_ready = sem("wbc_ready")
        v_made = sem("v_made")
        vsb_ready = sem("vsb_ready")
        xv_dve = sem("xv_dve")
        xv_pool = sem("xv_pool")
        x_turned = sem("x_turned")
        xT_ready = [sem(f"xT_ready{i}") for i in range(2)]
        f1_made = sem("f1_made")
        f1b_ready = sem("f1b_ready")
        f1n_made = sem("f1n_made")
        f1n_ready = sem("f1n_ready")
        f2raw_ready = sem("f2raw_ready")
        f2l_ready = sem("f2l_ready")
        nf2l_ready = sem("nf2l_ready")
        x2_ready = sem("x2_ready")
        x2_summed = sem("x2_summed")
        stat_ready = sem("stat_ready")
        stat_turned = sem("stat_turned")
        stmax_ready = sem("stmax_ready")
        diag_ready = sem("diag_ready")
        gst_made = sem("gst_made")
        gst_ready = sem("gst_ready")
        nF2_ready = sem("nF2_ready")
        rng_step = sem("rng_step")
        nat_in = [sem(f"nat_in{i}") for i in range(2)]
        exp_ready = sem("exp_ready")
        tab_step = sem("tab_step")
        rows_ready = sem("rows_ready")
        ea_ready = sem("ea_ready")
        y_ready = sem("y_ready")
        hi_ready = sem("hi_ready")
        table_ready = sem("table_ready")
        xsum_made = sem("xsum_made")
        xsum_ready = sem("xsum_ready")
        sign_ready = sem("sign_ready")
        cast_done = sem("cast_done")
        turn_done = sem("turn_done")
        first_plus = sem("first_plus")
        first_minus = sem("first_minus")
        plus_ready = sem("plus_ready")
        minus_ready = sem("minus_ready")
        sums_made = sem("sums_made")
        sums_out = sem("sums_out")
        sums_added = sem("sums_added")
        pool_step = sem("pool_step")
        rec_step = sem("rec_step")
        total_ready = sem("total_ready")
        y_done = sem("y_done")
        bn_step = sem("bn_step")
        mv_ready = sem("mv_ready")
        rstd_ready = sem("rstd_ready")
        out_ready = sem("out_ready")
        last_step = sem("last_step")
        last_ready = sem("last_ready")
        last_var_ready = sem("last_var_ready")
        last_rstd_ready = sem("last_rstd_ready")
        last_stored = sem("last_stored")
        out_stored = [sem(f"out_stored{i}") for i in range(2)]
        g_adj_in = sem("g_adj_in")
        g_xT_made = sem("g_xT_made")
        g_xT_ready = sem("g_xT_ready")
        g_f2_made = sem("g_f2_made")
        g_f2_ready = sem("g_f2_ready")
        g_step = sem("g_step")
        g_max_ready = sem("g_max_ready")
        g_exp_ready = sem("g_exp_ready")
        g_turned = sem("g_turned")
        g_pt_ready = sem("g_pt_ready")
        g_sum_made = sem("g_sum_made")
        g_out_ready = sem("g_out_ready")
        g_rstd = sem("g_rstd")
        g_stored = sem("g_stored")
        flag_ready = sem("flag_ready")

        steps_begun = {e.engine: sem(f"steps_begun_{n}") for n, e in
                       (("pe", nc.tensor), ("dve", nc.vector), ("pool", nc.gpsimd))}

        def xl_chunk(h):
            return xl.rearrange("p (n d) -> p n d", n=NK)[:, h * CN:(h + 1) * CN, :]

        def xv_chunk(h):
            return xv.rearrange("p (n d) -> p n d", n=NK)[:, h * CN:(h + 1) * CN, :]

        v2_rows = vsb[:, 2:3, :].to_broadcast([P, CN, D])

        block = ctx.enter_context(nc.Block())

        def fast(eng):
            eng.wait_ge(flag_ready, 1)
            return eng.value_load(flag[0:1, 0:1], min_val=0, max_val=1)

        def apart(eng):
            eng.sem_inc(steps_begun[eng.engine], 1)

        @block.sync
        def _(sp):
            port_order = (0, 2, 1, 3)
            sp.dma_start(wsb[:, :], W).then_inc(w_in, 16)
            for h in range(BCH):
                two = slice(h * NB // BCH, (h + 1) * NB // BCH)
                for a in port_order:
                    sp.dma_start(xl[a * SQ:(a + 1) * SQ, :].rearrange("r (b n) -> r b n", b=NB)[:, two],
                                 x_cols[a][:, two]).then_inc(xl_in[h], 16)

            def load_adj(t, slot):
                for a in port_order:
                    dst = nat[a * SQ:(a + 1) * SQ, slot, :].rearrange("s (g c) -> s g c", g=G)
                    sp.dma_start(dst, adj_v[t, a]).then_inc(nat_in[slot], 16)

            load_adj(0, 0)
            load_adj(1, 1)
            sp.dma_start(xn[:, :, :], x_rows).then_inc(xn_in, 16)
            for t in (2, 3):
                sp.wait_ge(cast_done, t - 1)
                load_adj(t, t % 2)
            go = fast(sp)
            with sp.If(go):
                def load_quad(q):
                    for c in range(QT):
                        sp.wait_ge(cast_done, QT * q + c - 1)
                        load_adj(QT * q + c, c % 2)

                def store(q, s):
                    sp.wait_ge(out_ready, q + 1)
                    sp.dma_start(out_q[q], ybt[:, s]).then_inc(out_stored[s], 16)

                load_quad(1)
                load_quad(2)
                load_quad(3)
                store(0, 0)
                with sp.Fori(2, NQ // 2) as turn:
                    load_quad(2 * turn)
                    store(2 * turn - 3, 1)
                    load_quad(2 * turn + 1)
                    store(2 * turn - 2, 0)
                store(NQ - 3, 1)
                store(NQ - 2, 0)
                for c in range(QT):
                    sp.wait_ge(last_ready, c + 1)
                    sp.dma_start(out_q[NQ - 1][:, c], post[:, 1, 0, c, 0:D]).then_inc(last_stored, 16)
                for s in range(2):
                    sp.wait_ge(out_stored[s], 16 * (NQ // 2 - s))
                sp.wait_ge(last_stored, 16 * QT)
            with sp.Else():
                def load_rows(t):
                    sp.dma_start(nat[:, 0, :], adj_t[t]).then_inc(g_adj_in, 16)

                def store_rows(t):
                    sp.wait_ge(g_out_ready, t + 1)
                    sp.dma_start(out_t[t], ybt[:, 1, 0, :]).then_inc(g_stored, 16)

                for s in range(2):
                    sp.wait_ge(nat_in[s], 2 * 16 * A)
                load_rows(0)
                with sp.Fori(1, NT) as t:
                    sp.wait_ge(g_max_ready, t)
                    load_rows(t)
                    store_rows(t - 1)
                store_rows(NT - 1)
                sp.wait_ge(g_stored, 16 * NT)
            sp.nop()

        @block.gpsimd
        def _(pool):
            pool.memset(ident[:, :], 0.0).then_inc(ident_zero, 1)
            pool.memset(ones[:, :], 1.0)
            pool.memset(mhalf[:, :], -0.5)
            pool.memset(xsum[:, D:DV], float(N))
            pool.wait_ge(ident_zero, 1)
            pool.affine_select(out=ident[:, :], in_=ident[:, :], compare_op=ALU.not_equal, fill=1.0,
                               base=0, pattern=[[-1, P]], channel_multiplier=1).then_inc(consts_ready, 1)
            pool.wait_ge(vsb_ready, 1)
            for h in (1, 3):
                pool.wait_ge(xl_in[h], 16 * A)
                pool.tensor_tensor(xv_chunk(h), xl_chunk(h), v2_rows, ALU.mult).then_inc(xv_pool, 1)
            for h in range(BCH):
                pool.wait_ge(f2raw_ready, h + 1)
                pool.wait_ge(xl_in[h], 16 * A)
                pool.tensor_tensor(x2[:, h].rearrange("p (n d) -> p n d", n=CN), xl_chunk(h), xl_chunk(h),
                                   ALU.mult).then_inc(x2_ready, 1)
            for i in range(2 * BCH):
                m, h = i // BCH, i % BCH
                part = slice(h * CN, (h + 1) * CN)
                pool.wait_ge(hi_ready, i + 1)
                pool.tensor_tensor(btv[m][:, part, DV:2 * DV], ybuf[:, h], btv[m][:, part, 0:DV],
                                   ALU.subtract).then_inc(table_ready, 1)
            go = fast(pool)
            with pool.If(go):
                PSTEPS = 4

                def quad(q, s):
                    pool.wait_ge(sums_out, QT * (q + 1))
                    pool.tensor_tensor(post[:, s, 0], post[:, s, 0], post[:, s, 1],
                                       ALU.add).then_inc(pool_step, 1)
                    pool.wait_ge(pool_step, PSTEPS * q + 1)
                    if not (isinstance(q, int) and q == 0):
                        pool.wait_ge(y_done, QT * q)
                    pool.tensor_tensor(ntot[:, :, :], post[:, s, 0, :, 0:DV], post[:, s, 0, :, DV:2 * DV],
                                       ALU.add).then_inc(sums_added, 1)
                    pool.wait_ge(rec_step, 3 * q + 3)
                    pool.wait_ge(xsum_ready, 1)
                    pool.tensor_tensor(isox[:, :, :], xsum[:, None, :].to_broadcast([P, QT, DV]),
                                       iso[:, :, None].to_broadcast([P, QT, DV]),
                                       ALU.mult).then_inc(pool_step, 1)
                    pool.wait_ge(pool_step, PSTEPS * q + 2)
                    pool.tensor_tensor(ntot[:, :, :], ntot[:, :, :], isox[:, :, :], ALU.add).then_inc(total_ready, 1)
                    pool.wait_ge(mv_ready, q + 1)
                    apart(pool)
                    pool.tensor_scalar(nmr[:, s], mv[:, s, :, 0], -1.0, None, ALU.mult)
                    pool.tensor_scalar(vpe[:, :], mv[:, s, :, 1], EPS, None, ALU.add).then_inc(pool_step, 1)
                    pool.wait_ge(pool_step, PSTEPS * q + 3)
                    pool.tensor_tensor(rstd[:, s], vpe[:, :], mhalf[:, :], ALU.pow).then_inc(pool_step, 1)
                    pool.wait_ge(pool_step, PSTEPS * q + 4)
                    pool.tensor_tensor(nmr[:, s], nmr[:, s], rstd[:, s], ALU.mult).then_inc(rstd_ready, 1)

                quad(0, 0)
                quad(1, 1)
                with pool.Fori(1, NQ // 2 - 1) as turn:
                    quad(2 * turn, 0)
                    quad(2 * turn + 1, 1)
                quad(NQ - 2, 0)
                for c in range(QT):
                    pool.wait_ge(last_var_ready, c + 1)
                    pool.tensor_tensor(rstd_l[:, c:c + 1], vpe_l[:, c:c + 1], mhalf[:, 0:1],
                                       ALU.pow).then_inc(last_rstd_ready, 1)
            with pool.Else():
                with pool.Fori(0, NT) as t:
                    pool.wait_ge(mv_ready, t + 1)
                    apart(pool)
                    pool.tensor_scalar(vpe[:, 0:1], mv[:, 0, 0, 1:2], EPS, None, ALU.add).then_inc(pool_step, 1)
                    pool.wait_ge(pool_step, t + 1)
                    pool.tensor_tensor(rstd[:, 0, 0:1], vpe[:, 0:1], mhalf[:, 0:1], ALU.pow).then_inc(g_rstd, 1)
            pool.nop()

        @block.scalar
        def _(act):
            act.dma_start(w12[:, 0:1], w1.rearrange("o h -> h o")).then_inc(w12_in, 16)
            act.dma_start(w12[:, 1:2], w2.rearrange("o h -> h o")).then_inc(w12_in, 16)
            act.dma_start(b12[:, 0:1], b1.partition_broadcast(P)).then_inc(b12_in, 16)
            act.dma_start(b12[:, 1:2], b2.partition_broadcast(P)).then_inc(b12_in, 16)

            def signs(q, s, b0, b1):
                for b in range(b0, b1):
                    for k in range(KB):
                        n = b * KB + k
                        ins = act.activation(sgn_b[s][:, b, :, k], f1b[:, bass.ds(q * QW, QW)], ACT.Sign,
                                             bias=nf2l[:, n:n + 1], scale=-1.0)
                    ins.then_inc(sign_ready, 1)

            def spread_out(b):
                act.wait_ge(f1_made, b + 1)
                act.activation(f1b[:, :].rearrange("p (a b r k) -> p b k a r", a=A, b=NB, r=SQ)[:, b],
                               ps[:, 4 + b % 2, :].rearrange("p (k a r) -> p k a r", k=KB, a=A), ACT.Identity,
                               bias=b12[:, 0:1]).then_inc(f1b_ready, 1)

            def split_x(i):
                m, h = i // BCH, i % BCH
                act.wait_ge(y_ready, i + 1)
                act.activation(btv[m][:, h * CN:(h + 1) * CN, 0:DV], ybuf[:, h], ACT.Copy).then_inc(hi_ready, 1)

            act.wait_ge(consts_ready, 1)
            act.activation(ac[:, 0, 0:1], ones[:, 0:1], ACT.Copy)
            for b in range(NXG):
                if b < NXG // 2:
                    act.wait_ge(x_turned, b + 1)
                    act.activation(xT[:, b * 512:(b + 1) * 512], ps[:, b % 4, :], ACT.Copy).then_inc(xT_ready[0], 1)
                if b == 1:
                    act.wait_ge(b12_in, 32)
                if b:
                    spread_out(b - 1)
                if b == QT:
                    act.wait_ge(f1b_ready, QT)
                    act.wait_ge(nf2l_ready, 1)
                    signs(0, 0, 0, 1)
                if b == QT + 1:
                    act.wait_ge(nF2_ready, 1)
                    act.activation(be[:, :], f2l[:, :], ACT.Exp, bias=nF2[:, 0:1]).then_inc(exp_ready, 1)
                    act.activation(de[:, :], f2l[:, :], ACT.Exp, scale=NEG_SLOPE).then_inc(exp_ready, 1)
            spread_out(NXG - 1)
            for i in range(2 * BCH):
                if i + 1 < NB:
                    signs(0, 0, i + 1, i + 2)
                split_x(i)
            go = fast(act)
            with act.If(go):
                def evacuate(q, s, c):
                    act.wait_ge(sums_made, QT * q + c + 1)
                    if c == 0 and not (isinstance(q, int) and q < 2):
                        act.wait_ge(sums_added, q - 1)
                    for m in range(2):
                        ins = act.activation(post[:, s, m, c, :], ps[:, 2 * (c % 2) + m, 0:2 * DV], ACT.Copy,
                                             scale=ac[:, m, bass.ds(QT * q + c, 1)])
                    ins.then_inc(sums_out, 1)

                def normalise(q, s):
                    act.wait_ge(rstd_ready, q + 1)
                    for c in range(QT):
                        ins = act.activation(ybt[:, s, c, :], ybt[:, s, c, :], ACT.Identity,
                                             bias=nmr[:, s, c:c + 1], scale=rstd[:, s, c:c + 1])
                    ins.then_inc(out_ready, 1)

                def quad(q, s, more=True, share=(0, 3, 6, NB, NB)):
                    for c in range(QT):
                        b0, b1 = share[c], share[c + 1]
                        if more and b1 > b0:
                            if c == 0:
                                if isinstance(q, int) and q == 0:
                                    act.wait_ge(x2_summed, 1)
                                else:
                                    act.wait_ge(minus_ready, 2 * q)
                            signs(q + 1, 1 - s, b0, b1)
                        if isinstance(q, int) and q == 0 and c == 0:
                            act.wait_ge(ea_ready, 1)
                            act.activation(ac[:, :, :], ea[:, :, :], ACT.Exp).then_inc(rows_ready, 1)
                            act.wait_ge(rows_ready, 1)
                        evacuate(q, s, c)
                        if c == 1 and not (isinstance(q, int) and q < 2):
                            normalise(q - 2, s)
                        if c == 2 and not more:
                            normalise(q - 1, 1 - s)

                quad(0, 0, share=(0, 2, 2, 6, NB))
                quad(1, 1)
                with act.Fori(1, NQ // 2 - 1) as turn:
                    quad(2 * turn, 0)
                    quad(2 * turn + 1, 1)
                quad(NQ - 2, 0)
                quad(NQ - 1, 1, more=False)
            with act.Else():
                P_nat = sgn[:, 0].bitcast(F32)
                with act.Fori(0, NT) as t:
                    act.wait_ge(g_max_ready, t + 1)
                    act.activation(P_nat, P_nat, ACT.Exp, bias=gnmax[:, 0:1],
                                   accum_out=gden[:, 0:1]).then_inc(g_exp_ready, 1)
            act.nop()

        @block.vector
        def _(dve):
            dve.wait_ge(w12_in, 32)
            dve.wait_ge(consts_ready, 1)
            for m in range(2):
                dve.tensor_scalar(wbc[:, m, :], ones[:, :], w12[:, m:m + 1], None, ALU.mult).then_inc(wbc_ready, 1)
            dve.wait_ge(v_made, 1)
            dve.tensor_copy(vsb[:, :, :].rearrange("p m n -> p (m n)"), ps[:, 6, 0:3 * P]).then_inc(vsb_ready, 1)
            def spread_stats(j, c0, c1):
                w = c1 - c0
                dve.wait_ge(stat_turned, j + 1)
                dve.tensor_reduce(stmax[0:w, j:j + 1], ps[0:w, 7, (1 + j) * P:(2 + j) * P], AX_X,
                                  ALU.max).then_inc(stmax_ready, 1)
                dve.wait_ge(stmax_ready, j + 1)
                dve.tensor_scalar(stdiag[0:w, c0:c1], ident[0:w, 0:w], stmax[0:w, j:j + 1], None,
                                  ALU.mult).then_inc(diag_ready, 1)
                dve.wait_ge(gst_made, j + 1)
                dve.tensor_copy(gst[:, c0:c1], ps[:, 7, 64 + c0:64 + c1]).then_inc(gst_ready, 1)
                dve.wait_ge(gst_ready, j + 1)

            def scale_x(i):
                m, h = i // BCH, i % BCH
                part = slice(h * CN, (h + 1) * CN)
                if i >= BCH:
                    dve.wait_ge(table_ready, i - BCH + 1)
                dve.tensor_copy(ybuf[:, h, :, D], cs[:, m, part])
                dve.tensor_tensor(ybuf[:, h, :, 0:D], xl_chunk(h),
                                  cs[:, m, part, None].to_broadcast([P, CN, D]),
                                  ALU.mult).then_inc(y_ready, 1)

            def edge_bytes(u, c):
                dve.wait_ge(nat_in[c], 16 * A * (u + 1))
                apart(dve)
                dve.tensor_scalar(mnt[:, 0, c * NK * P:(c + 1) * NK * P].bitcast(FP8), nat[:, c, :], 0,
                                  None, ALU.is_gt, saturate=False).then_inc(cast_done, 1)

            def turn_words(u, c):
                dve.wait_ge(cast_done, 2 * u + c + 1)
                dve.transpose(mt_w[:, :, c * P:(c + 1) * P].rearrange("p b (g s) -> p g b s", g=G),
                              mn_w[:, c * NK * SQ:(c + 1) * NK * SQ].rearrange("p (g b r) -> p g b r", g=G, b=NB)
                              ).then_inc(turn_done, 1)

            def plus(q, s, h, blocks):
                for b in blocks:
                    dve.wait_ge(sign_ready, NB * q + b + 1)
                    ins = dve.scalar_tensor_tensor(out=mask_w[h][0][:, b, :],
                                                   in0=sgn_w[s][:, b, h * PW:(h + 1) * PW],
                                                   scalar=pat[:, :].bitcast(U32)[:, b:b + 1],
                                                   in1=mt_w[:, b, :], op0=ALU.bitwise_and,
                                                   op1=ALU.bitwise_and)
                return ins

            def minus(s, h, b0=0, b1=NB):
                return dve.scalar_tensor_tensor(out=mask_w[h][1][:, b0:b1, :],
                                                in0=sgn_w[s][:, b0:b1, h * PW:(h + 1) * PW],
                                                scalar=0xFFFFFFFF, in1=mt_w[:, b0:b1, :],
                                                op0=ALU.bitwise_xor, op1=ALU.bitwise_and)

            def xv_product(h):
                dve.wait_ge(xl_in[h], 16 * A)
                dve.tensor_tensor(xv_chunk(h), xl_chunk(h), v2_rows, ALU.mult).then_inc(xv_dve, 1)

            def f2_sum(h):
                dve.wait_ge(xv_pool if h % 2 else xv_dve, h // 2 + 1)
                dve.tensor_reduce(f2raw[:, h * CN:(h + 1) * CN], xv_chunk(h), AX_X, ALU.add).then_inc(f2raw_ready, 1)

            def xT_out(b):
                dve.wait_ge(x_turned, b + 1)
                dve.tensor_copy(xT[:, b * 512:(b + 1) * 512], ps[:, b % 4, :]).then_inc(xT_ready[1], 1)

            dve.wait_ge(vsb_ready, 1)
            xv_product(0)
            f2_sum(0)
            xv_product(2)
            f2_sum(1)
            f2_sum(2)
            xT_out(4)
            f2_sum(3)
            dve.wait_ge(f2raw_ready, BCH)
            dve.wait_ge(b12_in, 32)
            dve.tensor_scalar(nf2l[:, :], f2raw[:, :], b12[:, 1:2], -1.0, ALU.add, ALU.mult).then_inc(nf2l_ready, 1)
            dve.tensor_scalar(f2l[:, :], f2raw[:, :], b12[:, 1:2], None, ALU.add).then_inc(f2l_ready, 1)
            dve.wait_ge(f2l_ready, 1)
            dve.tensor_reduce(stat[:, 0:1], f2l[:, :], AX_X, ALU.max)
            dve.tensor_reduce(stat[:, 1:2], f2l[:, :], AX_X, ALU.min, negate=True).then_inc(stat_ready, 1)
            xT_out(5)
            spread_stats(0, 0, 2)
            dve.tensor_scalar(nF2[:, :], gst[:, 0:1], -1.0, None, ALU.mult).then_inc(nF2_ready, 1)
            xT_out(6)
            xT_out(7)
            dve.wait_ge(exp_ready, 1)
            dve.tensor_scalar(p2[:, :].bitcast(I32), be[:, :].bitcast(I32), 0x7F800000, None,
                              ALU.bitwise_and).then_inc(tab_step, 1)
            dve.wait_ge(tab_step, 1)
            dve.tensor_scalar(p2[:, :], p2[:, :], PAT_MIN, None, ALU.max).then_inc(tab_step, 1)
            dve.wait_ge(tab_step, 2)
            dve.tensor_copy(pat[:, :], p2[:, :], saturate=False)
            dve.reciprocal(rp[:, :], p2[:, :]).then_inc(tab_step, 1)
            dve.wait_ge(tab_step, 3)
            dve.scalar_tensor_tensor(out=cs[:, 0, :], in0=be[:, :], scalar=SCALE, in1=rp[:, :],
                                     op0=ALU.mult, op1=ALU.mult).then_inc(tab_step, 1)
            dve.wait_ge(exp_ready, 2)
            dve.tensor_scalar(cs[:, 1, :], de[:, :], SCALE, None, ALU.mult).then_inc(tab_step, 1)
            dve.wait_ge(tab_step, 5)
            scale_x(0)
            edge_bytes(0, 0)
            scale_x(1)
            turn_words(0, 0)
            scale_x(2)
            edge_bytes(0, 1)
            turn_words(0, 1)
            scale_x(3)
            dve.wait_ge(turn_done, 2)
            dve.wait_ge(f1_made, NXG)
            for b in range(4):
                plus(0, 0, 0, [b]).then_inc(first_plus, 1)
            dve.wait_ge(f1n_made, 1)
            dve.tensor_copy(f1n[:, :], ps[:, 6, 0:NT]).then_inc(f1n_ready, 1)
            scale_x(4)
            minus(0, 0, 0, 4).then_inc(first_minus, 1)
            scale_x(5)
            dve.wait_ge(f1n_ready, 1)
            dve.tensor_reduce(stat[:, 2:3], f1n[:, :], AX_X, ALU.max,
                              apply_absolute_value=True).then_inc(stat_ready, 1)
            dve.wait_ge(x2_summed, 1)
            dve.tensor_reduce(gst[:, 3:4], ps[:, 5, :], AX_X, ALU.max)
            for b in range(4, 6):
                plus(0, 0, 0, [b]).then_inc(first_plus, 1)
            scale_x(6)
            spread_stats(1, 2, 3)
            dve.tensor_tensor(rng[:, 0:1], gst[:, 0:1], gst[:, 1:2], ALU.add).then_inc(rng_step, 1)
            dve.scalar_tensor_tensor(out=rng[:, 1:2], in0=gst[:, 0:1], scalar=gst[:, 1:2], in1=gst[:, 2:3],
                                     op0=ALU.max, op1=ALU.add).then_inc(rng_step, 1)
            plus(0, 0, 0, [6]).then_inc(first_plus, 1)
            dve.wait_ge(rng_step, 2)
            dve.tensor_scalar(rng[:, 2:3], rng[:, 0:1], F2_SPAN, None, ALU.is_le).then_inc(rng_step, 1)
            minus(0, 0, 4, 6).then_inc(first_minus, 1)
            dve.wait_ge(rng_step, 3)
            dve.scalar_tensor_tensor(out=rng[:, 3:4], in0=rng[:, 1:2], scalar=F_ABS, in1=rng[:, 2:3],
                                     op0=ALU.is_le, op1=ALU.mult).then_inc(rng_step, 1)
            scale_x(7)
            dve.wait_ge(rng_step, 4)
            dve.scalar_tensor_tensor(out=rng[:, 0:1], in0=gst[:, 3:4], scalar=X_MAX ** 2, in1=rng[:, 3:4],
                                     op0=ALU.is_le, op1=ALU.mult).then_inc(rng_step, 1)
            dve.tensor_scalar(gsum[:, :], f1n[:, :], gst[:, 0:1], None, ALU.add).then_inc(tab_step, 1)
            plus(0, 0, 0, [7]).then_inc(first_plus, 1)
            dve.wait_ge(tab_step, 6)
            dve.scalar_tensor_tensor(out=mrow[:, :], in0=gsum[:, :], scalar=NEG_SLOPE, in1=gsum[:, :],
                                     op0=ALU.mult, op1=ALU.max).then_inc(tab_step, 1)
            dve.wait_ge(rng_step, 5)
            dve.scalar_tensor_tensor(out=flag[:, :], in0=gst[:, 3:4], scalar=X_MIN ** 2 * N / KB, in1=rng[:, 0:1],
                                     op0=ALU.is_ge, op1=ALU.mult).then_inc(flag_ready, 1)
            minus(0, 0, 6, 8).then_inc(minus_ready, 1)
            dve.wait_ge(tab_step, 7)
            dve.tensor_tensor(ea[:, 0, :], gsum[:, :], mrow[:, :], ALU.subtract)
            dve.scalar_tensor_tensor(out=ea[:, 1, :], in0=f1n[:, :], scalar=NEG_SLOPE, in1=mrow[:, :],
                                     op0=ALU.mult, op1=ALU.subtract).then_inc(ea_ready, 1)
            dve.wait_ge(y_ready, 2 * BCH)
            go = fast(dve)
            with dve.If(go):
                def pair(u, q, s, h, between=None):
                    edge_bytes(u, 0)
                    edge_bytes(u, 1)
                    turn_words(u, 0)
                    turn_words(u, 1)
                    if between:
                        between()
                    dve.wait_ge(turn_done, 2 * u + 2)
                    if not (isinstance(u, int) and u < 2):
                        dve.wait_ge(sums_made, 2 * u - 2)
                    if isinstance(u, int) and u < EARLY:
                        for b in range(NB):
                            plus(q, s, h, [b]).then_inc(first_plus, 1)
                    else:
                        plus(q, s, h, range(NB)).then_inc(plus_ready, 1)
                    minus(s, h).then_inc(minus_ready, 1)

                def weights(q, s):
                    dve.wait_ge(sums_added, q + 1)
                    dve.tensor_scalar(iso[:, :], ntot[:, :, D], 0.0, None, ALU.is_equal).then_inc(rec_step, 1)
                    dve.wait_ge(rec_step, 3 * q + 1)
                    dve.scalar_tensor_tensor(out=den[:, :], in0=iso[:, :], scalar=float(N), in1=ntot[:, :, D],
                                             op0=ALU.mult, op1=ALU.add).then_inc(rec_step, 1)
                    dve.wait_ge(rec_step, 3 * q + 2)
                    dve.reciprocal(rec[:, :], den[:, :]).then_inc(rec_step, 1)

                def moments(q, s):
                    dve.wait_ge(total_ready, q + 1)
                    if not (isinstance(q, int) and q < 2):
                        dve.wait_ge(out_stored[s], 8 * (q - s))
                    apart(dve)
                    for c in range(QT):
                        dve.scalar_tensor_tensor(out=ybt[:, s, c, :], in0=ntot[:, c, 0:D], scalar=rec[:, c:c + 1],
                                                 in1=xn[:, bass.ds(QT * q + c, 1), :].rearrange("p o d -> p (o d)"),
                                                 op0=ALU.mult, op1=ALU.add).then_inc(y_done, 1)
                    dve.wait_ge(y_done, QT * (q + 1))
                    for c in range(QT):
                        dve.bn_stats(bns[:, s, c, :], ybt[:, s, c, :]).then_inc(bn_step, 1)
                    dve.wait_ge(bn_step, QT * (q + 1))
                    apart(dve)
                    for c in range(QT):
                        ins = dve.bn_aggr(mv[:, s, c, :], bns[:, s, c, :])
                    ins.then_inc(mv_ready, 1)

                def quad(q, s):
                    pair(2 * q, q, s, 0)
                    weights(q - 2, s)
                    pair(2 * q + 1, q, s, 1, between=lambda: moments(q - 2, s))

                pair(1, 0, 0, 1)
                pair(2, 1, 1, 0)
                dve.wait_ge(xsum_made, 1)
                dve.tensor_reduce(xsum[:, 0:D], ps[:, 4, :].rearrange("p (k d) -> p d k", d=D), AX_X,
                                  ALU.add).then_inc(xsum_ready, 1)
                pair(3, 1, 1, 1)
                quad(2, 0)
                quad(3, 1)
                with dve.Fori(2, NQ // 2) as turn:
                    quad(2 * turn, 0)
                    quad(2 * turn + 1, 1)

                q, s = NQ - 1, 1
                TAIL = 8

                def finish(c):
                    t = QT * q + c
                    done = TAIL * c

                    def step(ins):
                        nonlocal done
                        done += 1
                        ins.then_inc(last_step, 1)
                        dve.wait_ge(last_step, done)

                    dve.wait_ge(sums_out, t + 1)
                    step(dve.tensor_tensor(post[:, s, 0, c], post[:, s, 0, c], post[:, s, 1, c], ALU.add))
                    step(dve.tensor_tensor(post[:, s, 1, c, 0:DV], post[:, s, 0, c, 0:DV],
                                           post[:, s, 0, c, DV:2 * DV], ALU.add))
                    total, rows = post[:, s, 1, c, 0:DV], post[:, s, 0, c, 0:D]
                    step(dve.tensor_scalar(iso_l[:, c:c + 1], total[:, D:DV], 0.0, None, ALU.is_equal))
                    step(dve.scalar_tensor_tensor(out=total, in0=xsum[:, :], scalar=iso_l[:, c:c + 1], in1=total,
                                                  op0=ALU.mult, op1=ALU.add))
                    step(dve.reciprocal(rec_l[:, c:c + 1], total[:, D:DV]))
                    step(dve.scalar_tensor_tensor(out=rows, in0=total[:, 0:D], scalar=rec_l[:, c:c + 1],
                                                  in1=xn[:, t, :], op0=ALU.mult, op1=ALU.add))
                    step(dve.bn_stats(bns[:, s, c, :], rows))
                    step(dve.bn_aggr(mv[:, s, c, :], bns[:, s, c, :]))
                    dve.tensor_scalar(vpe_l[:, c:c + 1], mv[:, s, c, 1:2], EPS, None,
                                      ALU.add).then_inc(last_var_ready, 1)

                def normalise(c):
                    dve.wait_ge(last_rstd_ready, c + 1)
                    rows = post[:, s, 0, c, 0:D]
                    dve.tensor_scalar(rows, rows, mv[:, s, c, 0:1], rstd_l[:, c:c + 1],
                                      ALU.subtract, ALU.mult).then_inc(last_ready, 1)

                weights(NQ - 2, 0)
                finish(0)
                moments(NQ - 2, 0)
                finish(1)
                finish(2)
                for c in range(QT - 1):
                    normalise(c)
                finish(QT - 1)
                normalise(QT - 1)
            with dve.Else():
                f2r = bt[:, 0].bitcast(F32)[:, 0:N]
                z = bt[:, 1].bitcast(F32)[:, 0:N]
                s_nat = sgn[:, 0].bitcast(F32)
                pT = sgn[:, 1].bitcast(F32)
                dve.wait_ge(table_ready, 2 * BCH)
                for g in range(NXG):
                    dve.wait_ge(g_xT_made, g + 1)
                    dve.tensor_copy(xT[:, 0:512], ps[:, 3, :]).then_inc(g_xT_ready, 1)
                    dve.wait_ge(g_f2_made, g + 1)
                    dve.tensor_scalar(f2r[:, g * 512:(g + 1) * 512], ps[:, g % 2, :], b12[:, 1:2], None,
                                      ALU.add).then_inc(g_f2_ready, 1)
                dve.wait_ge(g_f2_ready, NXG)
                dve.wait_ge(xn_in, 16)
                STEPS = 7
                with dve.Fori(0, NT) as t:
                    dve.tensor_scalar(z, f2r, f1n[:, bass.ds(t, 1)], None, ALU.add).then_inc(g_step, 1)
                    dve.wait_ge(g_step, STEPS * t + 1)
                    dve.scalar_tensor_tensor(out=z, in0=z, scalar=NEG_SLOPE, in1=z, op0=ALU.mult,
                                             op1=ALU.max).then_inc(g_step, 1)
                    dve.wait_ge(g_adj_in, 16 * (t + 1))
                    dve.tensor_scalar(s_nat, nat[:, 0, :], 0, 1.0, ALU.is_gt, ALU.subtract).then_inc(g_step, 1)
                    dve.wait_ge(g_step, STEPS * t + 3)
                    dve.scalar_tensor_tensor(out=s_nat, in0=s_nat, scalar=NEG_INF, in1=z, op0=ALU.mult,
                                             op1=ALU.add).then_inc(g_step, 1)
                    dve.wait_ge(g_step, STEPS * t + 4)
                    dve.tensor_reduce(gnmax[:, 0:1], s_nat, AX_X, ALU.max, negate=True).then_inc(g_max_ready, 1)
                    for g in range(NXG):
                        dve.wait_ge(g_turned, NXG * t + g + 1)
                        dve.tensor_copy(pT[:, g * 512:(g + 1) * 512], ps[:, g % 2, :]).then_inc(g_pt_ready, 1)
                    dve.reciprocal(rec[:, 0:1], gden[:, 0:1]).then_inc(g_step, 1)
                    dve.wait_ge(g_step, STEPS * t + 5)
                    dve.wait_ge(g_sum_made, t + 1)
                    dve.scalar_tensor_tensor(out=ybt[:, 0, 0, :], in0=ps[:, 2, 0:D], scalar=rec[:, 0:1],
                                             in1=xn[:, bass.ds(t, 1), :].rearrange("p o d -> p (o d)"),
                                             op0=ALU.mult, op1=ALU.add).then_inc(g_step, 1)
                    dve.wait_ge(g_step, STEPS * t + 6)
                    dve.bn_stats(bns[:, 0, 0, :], ybt[:, 0, 0, :]).then_inc(g_step, 1)
                    dve.wait_ge(g_step, STEPS * t + 7)
                    apart(dve)
                    dve.bn_aggr(mv[:, 0, 0, :], bns[:, 0, 0, :]).then_inc(mv_ready, 1)
                    dve.wait_ge(g_rstd, t + 1)
                    dve.wait_ge(g_stored, 16 * t)
                    dve.tensor_scalar(ybt[:, 1, 0, :], ybt[:, 0, 0, :], mv[:, 0, 0, 0:1], rstd[:, 0, 0:1],
                                      ALU.subtract, ALU.mult).then_inc(g_out_ready, 1)
            dve.nop()

        @block.tensor
        def _(pe):
            pe.wait_ge(w_in, 16)
            for m in range(2):
                pe.wait_ge(wbc_ready, m + 1)
                pe.matmul(ps[:, 6, m * P:(m + 1) * P], wsb[:, :], wbc[:, m, :], start=True, stop=True)
            pe.matmul(ps[:, 6, 2 * P:3 * P], wbc[:, 1, :], wsb[:, :], start=True, stop=True).then_inc(v_made, 1)

            def spread_f1(b):
                half = b // (NXG // 2)
                pe.wait_ge(xT_ready[half], b - half * NXG // 2 + 1)
                if b >= 2:
                    pe.wait_ge(f1b_ready, b - 1)
                pe.matmul(ps[:, 4 + b % 2, :], vsb[:, 0, :], xT[:, b * 512:(b + 1) * 512],
                          start=True, stop=True).then_inc(f1_made, 1)

            def turn_stats(j, c0, c1):
                pe.wait_ge(stat_ready, j + 1)
                pe.transpose(ps[0:c1 - c0, 7, (1 + j) * P:(2 + j) * P], stat[:, c0:c1],
                             ident[:, :]).then_inc(stat_turned, 1)

            def widen_stats(j, c0, c1):
                pe.wait_ge(diag_ready, j + 1)
                pe.matmul(ps[:, 7, 64 + c0:64 + c1], ones[0:c1 - c0, :], stdiag[0:c1 - c0, c0:c1],
                          start=True, stop=True).then_inc(gst_made, 1)

            for b in range(NXG):
                pe.wait_ge(xl_in[b * BCH // NB], 16 * A)
                if b == 0:
                    pe.wait_ge(consts_ready, 1)
                if b >= 4:
                    pe.wait_ge(xT_ready[0], b - 3)
                for k in range(KB):
                    n = b * KB + k
                    ins = pe.transpose(ps[:, b % 4, k * P:(k + 1) * P], xl[:, n * D:(n + 1) * D], ident[:, :])
                ins.then_inc(x_turned, 1)
                if b == 1:
                    pe.wait_ge(vsb_ready, 1)
                if b:
                    spread_f1(b - 1)
                if b == 5:
                    turn_stats(0, 0, 2)
                    widen_stats(0, 0, 2)
            spread_f1(NXG - 1)
            pe.wait_ge(f1b_ready, NXG)
            for t in range(NT):
                ins = pe.transpose(ps[:, 6, t:t + 1], f1b[0:1, t * P:(t + 1) * P], ident[0:1, 0:1])
            ins.then_inc(f1n_made, 1)

            def sum_rows(b):
                ins = pe.matmul(ps[:, 4, :], ones[:, :], xl[:, b * 512:(b + 1) * 512], start=(b == 0),
                                stop=(b == NXG - 1))
                if b == NXG - 1:
                    ins.then_inc(xsum_made, 1)

            for b in range(NXG):
                sum_rows(b)
            ones_bf16 = ones.bitcast(BF16).rearrange("p (n two) -> p n two", two=2)[:, :, 1]
            for h in range(BCH):
                pe.wait_ge(x2_ready, h + 1)
                for i in range(CN // KB):
                    ins = pe.matmul(ps[:, 5, :], ones_bf16, x2[:, h, i * 512:(i + 1) * 512],
                                    start=(h == 0 and i == 0), stop=(h == BCH - 1 and i == CN // KB - 1))
            ins.then_inc(x2_summed, 1)

            def edge_sums(slot, c, m, n, start, stop):
                return pe.matmul(ps[:, 2 * c + m, 0:2 * DV],
                                 mask_f[slot][m][:, n // KB, n % KB, c * P:(c + 1) * P],
                                 btv[m][:, n, :], start=start, stop=stop)

            def first_plus_sums(b):
                pe.wait_ge(first_plus, b + 1)
                if b * KB % CN == 0:
                    pe.wait_ge(table_ready, b * KB // CN + 1)
                for c in range(2):
                    for k in range(KB):
                        n = b * KB + k
                        edge_sums(0, c, 0, n, n == 0, n == NK - 1)

            def first_minus_sums(h):
                pe.wait_ge(table_ready, BCH + h + 1)
                for c in range(2):
                    for n in range(h * CN, (h + 1) * CN):
                        ins = edge_sums(0, c, 1, n, n == 0, n == NK - 1)
                    if h == BCH - 1:
                        ins.then_inc(sums_made, 1)

            for b in range(5):
                first_plus_sums(b)
            turn_stats(1, 2, 3)
            widen_stats(1, 2, 3)
            first_plus_sums(5)
            pe.wait_ge(first_minus, 1)
            first_minus_sums(0)
            first_minus_sums(1)
            first_plus_sums(6)
            first_plus_sums(7)
            pe.wait_ge(first_minus, 2)
            first_minus_sums(2)
            pe.wait_ge(minus_ready, 1)
            first_minus_sums(3)
            go = fast(pe)
            with pe.If(go):
                def pair(u, slot):
                    for c in range(2):
                        pe.wait_ge(sums_out, 2 * u + c - 1)
                        apart(pe)
                        for m, ready in enumerate((plus_ready, minus_ready)):
                            if c == 0:
                                pe.wait_ge(ready, u + 1 if m else u - EARLY + 1)
                                apart(pe)
                            for n in range(NK):
                                ins = edge_sums(slot, c, m, n, n == 0, n == NK - 1)
                        ins.then_inc(sums_made, 1)

                def early_pair(u, slot):
                    for c in range(2):
                        pe.wait_ge(sums_out, 2 * u + c - 1)
                        for n in range(NK):
                            if c == 0 and n % KB == 0:
                                pe.wait_ge(first_plus, NB * u + n // KB + 1)
                            edge_sums(slot, c, 0, n, n == 0, n == NK - 1)
                        if c == 0:
                            pe.wait_ge(minus_ready, u + 1)
                        for n in range(NK):
                            ins = edge_sums(slot, c, 1, n, n == 0, n == NK - 1)
                        ins.then_inc(sums_made, 1)

                for u in range(1, EARLY):
                    early_pair(u, u % 2)
                pair(3, 1)
                with pe.Fori(2, NT // 4) as turn:
                    pair(2 * turn, 0)
                    pair(2 * turn + 1, 1)
            with pe.Else():
                for g in range(NXG):
                    pe.wait_ge(xn_in, 16)
                    for c in range(XG):
                        ins = pe.transpose(ps[:, 3, c * P:(c + 1) * P], xn[:, g * XG + c, :], ident[:, :])
                    ins.then_inc(g_xT_made, 1)
                    pe.wait_ge(g_xT_ready, g + 1)
                    if g >= 2:
                        pe.wait_ge(g_f2_ready, g - 1)
                    pe.matmul(ps[:, g % 2, :], vsb[:, 1, :], xT[:, 0:512], start=True, stop=True).then_inc(g_f2_made, 1)
                pe.wait_ge(g_f2_ready, NXG)
                P_nat = sgn[:, 0].bitcast(F32)
                pT = sgn[:, 1].bitcast(F32)
                with pe.Fori(0, NT) as t:
                    pe.wait_ge(g_exp_ready, t + 1)
                    for g in range(NXG):
                        if g >= 2:
                            pe.wait_ge(g_pt_ready, NXG * t + g - 1)
                        for c in range(XG):
                            j = g * XG + c
                            ins = pe.transpose(ps[:, g % 2, c * P:(c + 1) * P], P_nat[:, j * P:(j + 1) * P],
                                               ident[:, :])
                        ins.then_inc(g_turned, 1)
                    pe.wait_ge(g_pt_ready, NXG * t + NXG)
                    for j in range(NT):
                        ins = pe.matmul(ps[:, 2, 0:D], pT[:, j * P:(j + 1) * P], xn[:, j, :],
                                        start=(j == 0), stop=(j == NT - 1))
                    ins.then_inc(g_sum_made, 1)
            pe.nop()


_INS = ["x", "adj", "L0_gnn_W", "L0_gnn_w1", "L0_gnn_b1", "L0_gnn_w2", "L0_gnn_b2"]


def kernel(**inputs):
    import numpy as np
    import concourse.bacc as bacc
    from concourse.bass_utils import run_bass_kernel_spmd

    nc = bacc.Bacc("TRN2", target_bir_lowering=False, num_devices=1)
    arrays, args = {}, []
    for name in _INS:
        a = np.ascontiguousarray(inputs[name])
        arrays[f"in_{name}"] = a
        args.append(nc.dram_tensor(f"in_{name}", a.shape, mybir.dt.from_np(a.dtype), kind="ExternalInput").ap())
    out = nc.dram_tensor("out", inputs["x"].shape, F32, kind="ExternalOutput").ap()
    gat_kernel(nc, *args, out)
    r = run_bass_kernel_spmd(nc, [arrays], core_ids=[0])
    return r.results[0]["out"]
```
